# Optimizing a Trainium2 kernel written in Bass

```python
import numpy as np
import jax
import jax.numpy as jnp

def _softmax(x, axis=-1):
    return jax.nn.softmax(x, axis=axis)

def _gelu(x):
    return jax.nn.gelu(x, approximate=True)

def _silu(x):
    return jax.nn.silu(x)

def _sigmoid(x):
    return jax.nn.sigmoid(x)

def _layernorm(x, axis=-1, eps=1e-05):
    m = jnp.mean(x, axis=axis, keepdims=True)
    v = jnp.var(x, axis=axis, keepdims=True)
    return (x - m) / jnp.sqrt(v + eps)

def _scatter_add(tgt, idx, src, axis=0):
    return tgt.at[idx].add(src)

def _segment_sum(src, seg, n):
    return jax.ops.segment_sum(src, seg, n)
kernel_name = 'mk_adaln_ffn_d2_seqx_r8_b31419'

def setup_inputs(seed: int=0):
    np.random.seed(seed)
    _w = jnp.asarray

    def _rec_inputs():
        import jax
        import jax.numpy as jnp
        _rk = jax.random.key(seed)
        x = 0.0001734 + 0.8201 * jax.random.normal(jax.random.fold_in(_rk, 1), (64, 32, 512), jnp.float32)
        _lenS = 32 - jax.random.randint(jax.random.fold_in(_rk, 7), (64,), 0, max(1, 32 // 4) + 1, jnp.int32)
        _lenS2 = 32 - jax.random.randint(jax.random.fold_in(_rk, 8), (64,), 0, max(1, 32 // 4) + 1, jnp.int32)
        itok_B_0_7 = jax.random.randint(jax.random.fold_in(_rk, 11), (64,), 0, 8, jnp.int32)
        itok_B_2182_4065 = jax.random.randint(jax.random.fold_in(_rk, 13), (64,), 2182, 4066, jnp.int32)
        itok_Bx16_0_63 = jax.random.randint(jax.random.fold_in(_rk, 14), (64, 16), 0, 64, jnp.int32)
        itok_B_207_1644 = jax.random.randint(jax.random.fold_in(_rk, 15), (64,), 207, 1645, jnp.int32)
        return (x, itok_B_0_7, itok_B_2182_4065, itok_Bx16_0_63, itok_B_207_1644, _lenS)
    x, itok_B_0_7, itok_B_2182_4065, itok_Bx16_0_63, itok_B_207_1644, _lenS = _rec_inputs()

    def _L0_cond_setup():
        import jax, jax.numpy as jnp
        import numpy as np
        SESSION_CHANNELS = [128, 160, 192, 224, 240, 248, 252, 32]
        N_SESS = len(SESSION_CHANNELS)
        B, MAX_C, MAX_T = (16, 32, 512)
        HID, N_SRC = (64, 32)
        key = jax.random.key(seed)
        ks = jax.random.split(key, 7)
        session_ids = jax.random.randint(ks[0], (B,), 0, N_SESS)
        chan_table = jnp.asarray(SESSION_CHANNELS)
        channel_counts = chan_table[session_ids]
        seq_lens = jax.random.randint(ks[1], (B,), MAX_T // 2, MAX_T + 1)
        x = jax.random.normal(ks[2], (B, MAX_C, MAX_T), jnp.float32)
        cmask = (jnp.arange(MAX_C)[None, :] < channel_counts[:, None]).astype(x.dtype)
        tmask = (jnp.arange(MAX_T)[None, :] < seq_lens[:, None]).astype(x.dtype)
        x = x * cmask[:, :, None] * tmask[:, None, :]
        lim1 = 1.0 / np.sqrt(MAX_C)
        W_sess = jax.random.uniform(ks[3], (N_SESS, MAX_C, HID), jnp.float32, -lim1, lim1)
        b_sess = jax.random.uniform(ks[4], (N_SESS, HID), jnp.float32, -lim1, lim1)
        lim2 = 1.0 / np.sqrt(HID)
        W2 = jax.random.uniform(ks[5], (HID, N_SRC), jnp.float32, -lim2, lim2)
        b2 = jax.random.uniform(ks[6], (N_SRC,), jnp.float32, -lim2, lim2)
        return dict(x=x, session_ids=session_ids, channel_counts=channel_counts, seq_lens=seq_lens, W_sess=W_sess, b_sess=b_sess, W2=W2, b2=b2)
    _L0_cond_all = _L0_cond_setup()
    _L0_cond_in = {k: v for k, v in _L0_cond_all.items() if k in ('W_sess', 'b_sess', 'W2', 'b2')}
    del _L0_cond_all

    def _L0_ffn_setup():
        import jax, jax.numpy as jnp
        import numpy as np
        import math
        E, DK, R = (8, 32, 16)
        SCALING = 16.0 / 16.0
        key = jax.random.key(seed)
        ks = jax.random.split(key, 7)
        Bt, S, Din, Dout = (4, 256, 512, 512)
        x = jax.random.normal(ks[0], (Bt, S, Din), jnp.float32)
        W = jax.random.normal(ks[1], (Dout, Din), jnp.float32) * 0.02
        b = jnp.zeros((Dout,), jnp.float32)
        Wq = jax.random.normal(ks[2], (E * DK, Din), jnp.float32) * 0.02
        Wk = jax.random.normal(ks[3], (E * DK, Din), jnp.float32) * 0.02
        A = jax.random.normal(ks[4], (E, R, Din), jnp.float32) * 0.02
        Bm = jax.random.normal(ks[5], (E, Dout, R), jnp.float32) * 0.02
        return {'x': x, 'W': W, 'b': b, 'Wq': Wq, 'Wk': Wk, 'A': A, 'Bm': Bm}
    _L0_ffn_all = _L0_ffn_setup()
    _L0_ffn_in = {k: v for k, v in _L0_ffn_all.items() if k in ('W', 'b', 'Wq', 'Wk', 'A', 'Bm')}
    del _L0_ffn_all

    def _L1_cond_setup():
        import jax, jax.numpy as jnp
        import numpy as np
        B, S, HID = (4, 128, 512)
        D, HQ, HK = (128, 32, 8)
        PAGES, PSIZE, NPP = (64, 32, 16)
        THETA = 10000.0
        EPS = 1e-06
        SCALE = 1.0 / float(np.sqrt(D))

        def _rmsnorm(t, w):
            var = jnp.mean(t * t, axis=-1, keepdims=True)
            return t * jax.lax.rsqrt(var + EPS) * w

        def _rope(t, pos):
            inv_freq = 1.0 / THETA ** (jnp.arange(0, D, 2, dtype=jnp.float32) / D)
            freqs = pos[..., None].astype(jnp.float32) * inv_freq
            cos = jnp.cos(freqs)[:, :, None, :]
            sin = jnp.sin(freqs)[:, :, None, :]
            t1, t2 = (t[..., :D // 2], t[..., D // 2:])
            return jnp.concatenate([t1 * cos - t2 * sin, t2 * cos + t1 * sin], axis=-1)
        key = jax.random.key(seed)
        ks = jax.random.split(key, 10)
        x = jax.random.normal(ks[0], (B, S, HID), jnp.float32)
        Wq = jax.random.normal(ks[1], (HQ * D, HID), jnp.float32) * 0.02
        Wk = jax.random.normal(ks[2], (HK * D, HID), jnp.float32) * 0.02
        Wv = jax.random.normal(ks[3], (HK * D, HID), jnp.float32) * 0.02
        Wo = jax.random.normal(ks[4], (HID, HQ * D), jnp.float32) * 0.02
        q_norm_w = jax.random.uniform(ks[5], (D,), jnp.float32)
        k_norm_w = jax.random.uniform(ks[6], (D,), jnp.float32)
        k_cache = jax.random.normal(ks[7], (PAGES, PSIZE, HK, D), jnp.float32)
        v_cache = jax.random.normal(ks[8], (PAGES, PSIZE, HK, D), jnp.float32)
        block_table = jnp.arange(B * NPP, dtype=jnp.int32).reshape(B, NPP)
        cache_seqlens = jax.random.randint(ks[9], (B,), 0, 475).astype(jnp.int32)
        return dict(x=x, Wq=Wq, Wk=Wk, Wv=Wv, Wo=Wo, q_norm_w=q_norm_w, k_norm_w=k_norm_w, k_cache=k_cache, v_cache=v_cache, block_table=block_table, cache_seqlens=cache_seqlens)
    _L1_cond_all = _L1_cond_setup()
    _L1_cond_in = {k: v for k, v in _L1_cond_all.items() if k in ('Wq', 'Wk', 'Wv', 'Wo', 'q_norm_w', 'k_norm_w', 'k_cache', 'v_cache')}
    del _L1_cond_all

    def _L1_ffn_setup():
        import jax, jax.numpy as jnp
        import numpy as np

        @jax.custom_vjp
        def ste_sign(w):
            return jnp.sign(w)

        def _ste_fwd(w):
            return (jnp.sign(w), w)

        def _ste_bwd(w, g):
            mask = ((w > -1) & (w < 1)).astype(g.dtype)
            return (g * mask,)
        ste_sign.defvjp(_ste_fwd, _ste_bwd)
        key = jax.random.key(seed)
        k = jax.random.split(key, 6)
        B, S, H, O, E = (4, 256, 512, 512, 8)
        return {'x': jax.random.normal(k[0], (B, S, H), dtype=jnp.float32), 'weight': jax.random.normal(k[1], (O, H), dtype=jnp.float32) * 0.02, 'bias': jax.random.normal(k[2], (O,), dtype=jnp.float32) * 0.02, 'gate_w': jax.random.normal(k[3], (E, H), dtype=jnp.float32) * 0.02, 'in_channel_scale': jax.random.normal(k[4], (E, H), dtype=jnp.float32), 'out_channel_scale': jax.random.normal(k[5], (E, O), dtype=jnp.float32)}
    _L1_ffn_all = _L1_ffn_setup()
    _L1_ffn_in = {k: v for k, v in _L1_ffn_all.items() if k in ('weight', 'bias', 'gate_w', 'in_channel_scale', 'out_channel_scale')}
    del _L1_ffn_all
    return {'x': x, 'itok_B_0_7': itok_B_0_7, 'itok_B_2182_4065': itok_B_2182_4065, 'itok_Bx16_0_63': itok_Bx16_0_63, 'itok_B_207_1644': itok_B_207_1644, '_lenS': _lenS, 'L0_cond_W_sess': _L0_cond_in['W_sess'], 'L0_cond_b_sess': _L0_cond_in['b_sess'], 'L0_cond_W2': _L0_cond_in['W2'], 'L0_cond_b2': _L0_cond_in['b2'], 'L0_ffn_W': _L0_ffn_in['W'], 'L0_ffn_b': _L0_ffn_in['b'], 'L0_ffn_Wq': _L0_ffn_in['Wq'], 'L0_ffn_Wk': _L0_ffn_in['Wk'], 'L0_ffn_A': _L0_ffn_in['A'], 'L0_ffn_Bm': _L0_ffn_in['Bm'], 'L1_cond_Wq': _L1_cond_in['Wq'], 'L1_cond_Wk': _L1_cond_in['Wk'], 'L1_cond_Wv': _L1_cond_in['Wv'], 'L1_cond_Wo': _L1_cond_in['Wo'], 'L1_cond_q_norm_w': _L1_cond_in['q_norm_w'], 'L1_cond_k_norm_w': _L1_cond_in['k_norm_w'], 'L1_cond_k_cache': _L1_cond_in['k_cache'], 'L1_cond_v_cache': _L1_cond_in['v_cache'], 'L1_ffn_weight': _L1_ffn_in['weight'], 'L1_ffn_bias': _L1_ffn_in['bias'], 'L1_ffn_gate_w': _L1_ffn_in['gate_w'], 'L1_ffn_in_channel_scale': _L1_ffn_in['in_channel_scale'], 'L1_ffn_out_channel_scale': _L1_ffn_in['out_channel_scale']}

def reference(x, itok_B_0_7, itok_B_2182_4065, itok_Bx16_0_63, itok_B_207_1644, _lenS, L0_cond_W_sess, L0_cond_b_sess, L0_cond_W2, L0_cond_b2, L0_ffn_W, L0_ffn_b, L0_ffn_Wq, L0_ffn_Wk, L0_ffn_A, L0_ffn_Bm, L1_cond_Wq, L1_cond_Wk, L1_cond_Wv, L1_cond_Wo, L1_cond_q_norm_w, L1_cond_k_norm_w, L1_cond_k_cache, L1_cond_v_cache, L1_ffn_weight, L1_ffn_bias, L1_ffn_gate_w, L1_ffn_in_channel_scale, L1_ffn_out_channel_scale):
    import jax
    import jax.numpy as jnp

    def _L0_cond_ref(x, session_ids, channel_counts, seq_lens, W_sess, b_sess, W2, b2):
        import jax, jax.numpy as jnp
        import numpy as np
        SESSION_CHANNELS = [128, 160, 192, 224, 240, 248, 252, 32]
        N_SESS = len(SESSION_CHANNELS)
        B, MAX_C, MAX_T = (16, 32, 512)
        HID, N_SRC = (64, 32)
        cmask = (jnp.arange(x.shape[1])[None, :] < channel_counts[:, None]).astype(x.dtype)
        xm = x * cmask[:, :, None]
        W = W_sess[session_ids]
        b = b_sess[session_ids]
        h = jnp.einsum('bct,bch->bht', xm, W) + b[:, :, None]
        h = jax.nn.gelu(h, approximate=False)
        out = jnp.einsum('bht,hs->bst', h, W2) + b2[None, :, None]
        tmask = (jnp.arange(x.shape[2])[None, :] < seq_lens[:, None]).astype(x.dtype)
        return out * tmask[:, None, :]

    def _L0_ffn_ref(x, W, b, Wq, Wk, A, Bm):
        import jax, jax.numpy as jnp
        import numpy as np
        import math
        E, DK, R = (8, 32, 16)
        SCALING = 16.0 / 16.0
        Bt, S, Din = x.shape
        result = jnp.einsum('bsi,oi->bso', x, W) + b
        q = jnp.einsum('bsi,ni->bsn', x, Wq).reshape(Bt, S, E, DK)
        k = jnp.einsum('bsi,ni->bsn', x, Wk).reshape(Bt, S, E, DK)
        scores = jnp.einsum('bsed,bsed->bse', q, k) / math.sqrt(DK)
        w = jax.nn.softmax(scores, axis=-1)
        h = jnp.einsum('bsi,eri->bser', x, A)
        combined = jnp.einsum('bse,bser,eor->bso', w, h, Bm) * SCALING
        return result + combined

    def _L1_cond_ref(x, Wq, Wk, Wv, Wo, q_norm_w, k_norm_w, k_cache, v_cache, block_table, cache_seqlens):
        import jax, jax.numpy as jnp
        import numpy as np
        B, S, HID = (4, 128, 512)
        D, HQ, HK = (128, 32, 8)
        PAGES, PSIZE, NPP = (64, 32, 16)
        THETA = 10000.0
        EPS = 1e-06
        SCALE = 1.0 / float(np.sqrt(D))

        def _rmsnorm(t, w):
            var = jnp.mean(t * t, axis=-1, keepdims=True)
            return t * jax.lax.rsqrt(var + EPS) * w

        def _rope(t, pos):
            inv_freq = 1.0 / THETA ** (jnp.arange(0, D, 2, dtype=jnp.float32) / D)
            freqs = pos[..., None].astype(jnp.float32) * inv_freq
            cos = jnp.cos(freqs)[:, :, None, :]
            sin = jnp.sin(freqs)[:, :, None, :]
            t1, t2 = (t[..., :D // 2], t[..., D // 2:])
            return jnp.concatenate([t1 * cos - t2 * sin, t2 * cos + t1 * sin], axis=-1)
        bsz, seqlen, _ = x.shape
        q = jnp.einsum('bsd,ed->bse', x, Wq).reshape(bsz, seqlen, HQ, D)
        k = jnp.einsum('bsd,ed->bse', x, Wk).reshape(bsz, seqlen, HK, D)
        v = jnp.einsum('bsd,ed->bse', x, Wv).reshape(bsz, seqlen, HK, D)
        q = _rmsnorm(q, q_norm_w)
        k = _rmsnorm(k, k_norm_w)
        pos = cache_seqlens[:, None] + jnp.arange(seqlen)[None, :]
        q = _rope(q, pos)
        k = _rope(k, pos)
        L = NPP * PSIZE
        kc = k_cache[block_table].reshape(bsz, L, HK, D)
        vc = v_cache[block_table].reshape(bsz, L, HK, D)
        k_all = jnp.concatenate([kc, k], axis=1)
        v_all = jnp.concatenate([vc, v], axis=1)
        valid_c = jnp.arange(L)[None, :] < cache_seqlens[:, None]
        valid = jnp.concatenate([valid_c, jnp.ones((bsz, seqlen), dtype=bool)], axis=1)
        rep = HQ // HK
        k_all = jnp.repeat(k_all, rep, axis=2)
        v_all = jnp.repeat(v_all, rep, axis=2)
        scores = jnp.einsum('bqhd,bkhd->bhqk', q, k_all) * SCALE
        scores = jnp.where(valid[:, None, None, :], scores, -1e+30)
        probs = jax.nn.softmax(scores, axis=-1)
        o = jnp.einsum('bhqk,bkhd->bqhd', probs, v_all)
        o = o.reshape(bsz, seqlen, HQ * D)
        return jnp.einsum('bse,de->bsd', o, Wo)

    def _L1_ffn_ref(x, weight, bias, gate_w, in_channel_scale, out_channel_scale):
        import jax, jax.numpy as jnp
        import numpy as np

        @jax.custom_vjp
        def ste_sign(w):
            return jnp.sign(w)

        def _ste_fwd(w):
            return (jnp.sign(w), w)

        def _ste_bwd(w, g):
            mask = ((w > -1) & (w < 1)).astype(g.dtype)
            return (g * mask,)
        ste_sign.defvjp(_ste_fwd, _ste_bwd)
        B, S, H = x.shape
        xf = x.reshape(-1, H)
        router_logits = xf @ gate_w.T
        routing = jax.nn.softmax(router_logits.astype(jnp.float32), axis=1).astype(x.dtype)
        in_scale = routing @ in_channel_scale
        out_scale = routing @ out_channel_scale
        wb = ste_sign(weight)
        out = xf * in_scale @ wb.T * out_scale + bias
        return out.reshape(B, S, -1)
    x = x + _L0_ffn_ref(_L0_cond_ref(x, itok_B_0_7, _lenS, itok_B_2182_4065, L0_cond_W_sess, L0_cond_b_sess, L0_cond_W2, L0_cond_b2), L0_ffn_W, L0_ffn_b, L0_ffn_Wq, L0_ffn_Wk, L0_ffn_A, L0_ffn_Bm)
    x = x + _L1_ffn_ref(_L1_cond_ref(x, L1_cond_Wq, L1_cond_Wk, L1_cond_Wv, L1_cond_Wo, L1_cond_q_norm_w, L1_cond_k_norm_w, L1_cond_k_cache, L1_cond_v_cache, itok_Bx16_0_63, itok_B_207_1644), L1_ffn_weight, L1_ffn_bias, L1_ffn_gate_w, L1_ffn_in_channel_scale, L1_ffn_out_channel_scale)
    return x

_drawn_inputs = setup_inputs


def setup_inputs(seed=0):
    import zlib

    import numpy as np

    out = dict(_drawn_inputs(seed))
    spreads = {'L0_ffn_b': (0.0, 0.1)}
    factors = {'L0_cond_b_sess': 3.179,
     'L0_ffn_Wq': 8.0,
     'L0_ffn_Wk': 8.0,
     'L0_ffn_A': 8.0,
     'L0_ffn_Bm': 8.0,
     'L1_cond_Wk': 8.0,
     'L1_cond_k_norm_w': 8.0,
     'L1_ffn_gate_w': 5.328,
     'L1_ffn_bias': 3.234}
    for name, (base, spread) in spreads.items():
        noise = np.random.default_rng([zlib.crc32(name.encode()), seed]).standard_normal(out[name].shape)
        drawn = base * np.exp(spread * noise) if base else spread * noise
        out[name] = jnp.asarray(drawn.astype(out[name].dtype))
    for name, factor in factors.items():
        out[name] = (out[name] * factor).astype(out[name].dtype)
    return out
```

```python
import math
from contextlib import ExitStack

import numpy as np

import concourse.bass as bass
from concourse import mybir

F32 = mybir.dt.float32
F32R = mybir.dt.float32r
I32 = mybir.dt.int32
ALU = mybir.AluOpType
ACT = mybir.ActivationFunctionType
AX = mybir.AxisListType

P = 128
B, S, D = 64, 32, 512
BT = P // S
NT = B // BT
DC = D // P
HID = 64
NE, DK, RANK = 8, 32, 16
HQ, HK, HD = 32, 8, 128
REP = HQ // HK
PAGES, PSIZE, NPP = 64, 32, 16
L = NPP * PSIZE
G4 = 4
THETA, EPS = 10000.0, 1e-6
SCALE = 1.0 / math.sqrt(HD)
MASKED = -1e30
BIG = 3e38
PI2_A = 6.28125
PI2_B = 4058 / 2**21
PI2_C = 2 * math.pi - PI2_A - PI2_B
ROUND = 12582912.0


def started(turn):
    return not (isinstance(turn, int) and turn == 0)


def split3(pe, out, lhs, rhs, start, stop):
    pe.matmul(out, lhs[0], rhs[0], start=start, stop=False)
    pe.matmul(out, lhs[0], rhs[1], start=False, stop=False)
    return pe.matmul(out, lhs[1], rhs[0], start=False, stop=stop)


def constants(nc, t, d):
    with ExitStack() as ctx:
        def sb(name, shape, dt=F32):
            return ctx.enter_context(nc.sbuf_tensor(name, shape, dt))

        def sem(name):
            return ctx.enter_context(nc.semaphore(name))

        ids_i = sb("ids_i", [1, B], I32)
        counts_i = sb("counts_i", [P, B], I32)
        table_i = sb("table_i", [P, B * NPP], I32)
        count_f = sb("count_f", [P, NT])
        chan_i = sb("chan_i", [P, 1], I32)
        chan_f = sb("chan_f", [P, 1])
        seen = sb("seen", [P, NT])
        frames_i = sb("frames_i", [P, B], I32)
        frames_f = sb("frames_f", [P, B])
        time_i = sb("time_i", [P, DC], I32)
        time_f = sb("time_f", [P, DC])
        cached_i = sb("cached_i", [P, B], I32)
        start_f = sb("start_f", [P, NT])
        pos = sb("pos", [P, NT])
        freq = sb("freq", [P, HD // 2])
        qw = sb("qw", [P, HD])
        kw = sb("kw", [P, HD])
        angle = sb("angle", [P, NT, HD // 2])
        turn = sb("turn", [P, NT, HD // 2])
        part = sb("part", [P, NT, HD // 2])
        sin_t = sb("sin_t", [P, NT, HD // 2])
        cos_t = sb("cos_t", [P, NT, HD // 2])
        pages_f = sb("pages_f", [P, B, G4])
        lane_f = sb("lane_f", [P, 1])
        key_i = sb("key_i", [P, L], I32)

        loaded = sem("c_loaded")
        ids_in = sem("c_ids_in")
        session_in = sem("c_session_in")
        zeroed = sem("c_zeroed")
        made = sem("c_made")
        step = sem("c_step")
        sines = sem("c_sines")

        block = ctx.enter_context(nc.Block())
        n_loads = [0]
        angles_at = []

        @block.sync
        def _(sp):
            sp.dma_start(ids_i[:], d["ids"].rearrange("(o b) -> o b", o=1)).then_inc(ids_in, 16)

            def load(dst, src):
                n_loads[0] += 1
                sp.dma_start(dst, src).then_inc(loaded, 16)

            for dst, src in ((counts_i, d["counts"]), (table_i, d["table"]), (frames_i, d["frames"]), (cached_i, d["cached"]), (freq, d["freq"]),
                             (qw, d["qw"]), (kw, d["kw"])):
                load(dst[:], src.rearrange("(o n) -> o n", o=1).to_broadcast([P, src.shape[0]]))
            load(t["bias0"][:], d["b0"].rearrange("(o n) -> o n", o=1).to_broadcast([P, D]))
            load(t["b2"][:], d["b2"].rearrange("(o n) -> o n", o=1).to_broadcast([P, S]))
            sp.wait_ge(ids_in, 16)
            sp.wait_ge(zeroed, 2)
            with sp.Fori(0, NT) as tile:
                for j in range(BT):
                    sid = sp.value_load(ids_i[0:1, bass.ds(tile * BT + j, 1)], min_val=0, max_val=7)
                    half = slice((j % 2) * HID, (j % 2 + 1) * HID)
                    sp.dma_start(t["wsel"][j * S:(j + 1) * S, bass.ds(tile, 1), j // 2, half],
                                 d["w_sess"][bass.ds(sid, 1), :, :].rearrange("a c h -> c a h")).then_inc(session_in, 16)
                    with nc.allow_non_contiguous_dma(reason="64 biases of a session"):
                        sp.dma_start(t["bsel"][half, bass.ds(tile, 1), j // 2:j // 2 + 1],
                                     d["b_sess"][bass.ds(sid, 1), :].rearrange("a (h o) -> h a o", o=1))\
                            .then_inc(session_in, 16)
            for i in range(2):
                sp.dma_start(t["w2"][i * HID:(i + 1) * HID, i * S:(i + 1) * S], d["w2"]).then_inc(session_in, 16)

        @block.gpsimd
        def _(pool):
            nc.gpsimd.memset(t["wsel"][:], 0.0).then_inc(zeroed, 1)
            nc.gpsimd.memset(t["w2"][:], 0.0).then_inc(zeroed, 1)
            nc.gpsimd.memset(t["ident"][:], 0.0).then_inc(made, 1)
            nc.gpsimd.iota(chan_i[:], pattern=[[0, 1]], base=0, channel_multiplier=1).then_inc(made, 1)
            nc.gpsimd.iota(time_i[:], pattern=[[P, DC]], base=0, channel_multiplier=1).then_inc(made, 1)
            nc.gpsimd.iota(key_i[:], pattern=[[1, L]], base=0, channel_multiplier=0).then_inc(made, 1)
            pool.wait_ge(made, 4)
            nc.gpsimd.affine_select(out=t["ident"][:], in_=t["ident"][:], compare_op=ALU.not_equal, fill=1.0,
                                    base=0, pattern=[[-1, P]], channel_multiplier=1).then_inc(made, 1)

        @block.vector
        def _(dve):
            done = [0]

            def then(ins):
                done[0] += 1
                ins.then_inc(step, 1)
                dve.wait_ge(step, done[0])

            dve.wait_ge(made, 5)
            dve.wait_ge(loaded, 16 * n_loads[0])
            then(nc.vector.tensor_scalar(chan_i[:], chan_i[:], S - 1, None, ALU.bitwise_and))
            then(nc.vector.tensor_copy(chan_f[:], chan_i[:]))
            for j in range(BT):
                rows = slice(j * S, (j + 1) * S)
                then(nc.vector.tensor_copy(count_f[rows, :], counts_i[rows, :].rearrange("p (t j) -> p t j", j=BT)[:, :, j]))
                then(nc.vector.tensor_copy(start_f[rows, :], cached_i[rows, :].rearrange("p (t j) -> p t j", j=BT)[:, :, j]))
                then(nc.vector.tensor_copy(pages_f[rows, :, :],
                                           table_i[rows, :].rearrange("p (b c j) -> p b c j", j=G4, b=B)[:, :, :, j]))
            then(nc.vector.tensor_scalar(seen[:], count_f[:], chan_f[:, 0:1], None, ALU.is_gt))
            then(nc.vector.tensor_copy(time_f[:], time_i[:]))
            then(nc.vector.tensor_copy(frames_f[:], frames_i[:]))
            for c in range(DC):
                then(nc.vector.tensor_scalar(t["tmask"][:, c, :], frames_f[:], time_f[:, c:c + 1], None, ALU.is_gt))
            then(nc.vector.tensor_copy(t["cached"][:], cached_i[:]))
            then(nc.vector.tensor_copy(t["key_no"][:], key_i[:]))
            then(nc.vector.tensor_scalar(pages_f[:], pages_f[:], float(PSIZE), chan_f[:, 0:1], ALU.mult, ALU.add))
            then(nc.vector.tensor_copy(t["vrows"][:], pages_f[:]))
            then(nc.vector.tensor_scalar(pos[:], start_f[:], chan_f[:, 0:1], None, ALU.add))
            then(nc.vector.tensor_tensor(angle[:], pos[:].unsqueeze(2).to_broadcast([P, NT, HD // 2]),
                                         freq[:].unsqueeze(1).to_broadcast([P, NT, HD // 2]), ALU.mult))
            for quarter, out in ((0.0, sin_t), (0.25, cos_t)):
                then(nc.vector.tensor_scalar(turn[:], angle[:], 1 / (2 * math.pi), quarter, ALU.mult, ALU.add))
                then(nc.vector.tensor_scalar(turn[:], turn[:], ROUND, None, ALU.add))
                then(nc.vector.tensor_scalar(turn[:], turn[:], ROUND, None, ALU.subtract))
                then(nc.vector.scalar_tensor_tensor(out=part[:], in0=turn[:], scalar=-PI2_A, in1=angle[:],
                                                    op0=ALU.mult, op1=ALU.add))
                then(nc.vector.scalar_tensor_tensor(out=part[:], in0=turn[:], scalar=-PI2_B, in1=part[:],
                                                    op0=ALU.mult, op1=ALU.add))
                then(nc.vector.scalar_tensor_tensor(out=part[:], in0=turn[:], scalar=-PI2_C, in1=part[:],
                                                    op0=ALU.mult, op1=ALU.add))
                then(nc.vector.tensor_scalar(part[:], part[:], quarter * 2 * math.pi, 3.1415925, ALU.add, ALU.min))
                then(nc.vector.tensor_scalar(out[:], part[:], -3.1415925, None, ALU.max))
            angles_at.append(done[0])
            dve.wait_ge(sines, 2)
            half = HD // 2
            for w, ca, sa in ((qw, t["cosq"], t["sinq"]), (kw, t["cosk"], t["sink"])):
                w1 = w[:, 0:half].unsqueeze(1).to_broadcast([P, NT, half])
                w2 = w[:, half:HD].unsqueeze(1).to_broadcast([P, NT, half])
                then(nc.vector.tensor_tensor(ca[:, :, 0:half], cos_t[:], w1, ALU.mult))
                then(nc.vector.tensor_tensor(ca[:, :, half:HD], cos_t[:], w2, ALU.mult))
                then(nc.vector.tensor_tensor(sa[:, :, half:HD], sin_t[:], w1, ALU.mult))
                then(nc.vector.tensor_tensor(part[:], sin_t[:], w2, ALU.mult))
                then(nc.vector.tensor_scalar(sa[:, :, 0:half], part[:], -1.0, None, ALU.mult))
            dve.wait_ge(session_in, 16 * (2 * B + 2))
            then(nc.vector.tensor_tensor(t["wsel"][:].rearrange("p t j h -> p t (j h)"),
                                         t["wsel"][:].rearrange("p t j h -> p t (j h)"),
                                         seen[:].unsqueeze(2).to_broadcast([P, NT, 2 * P]), ALU.mult))

        @block.scalar
        def _(act):
            act.wait_ge(step, angles_at[0])
            nc.scalar.activation(sin_t[:], sin_t[:], ACT.Sin).then_inc(sines, 1)
            nc.scalar.activation(cos_t[:], cos_t[:], ACT.Sin).then_inc(sines, 1)


def layer0(nc, t, d):
    with ExitStack() as ctx:
        def sb(name, shape, dt=F32):
            return ctx.enter_context(nc.sbuf_tensor(name, shape, dt))

        def ps(name, shape):
            return ctx.enter_context(nc.psum_tensor(name, shape, F32))

        def sem(name):
            return ctx.enter_context(nc.semaphore(name))

        w0 = sb("w0", [P, DC, D])
        wqk = sb("wqk", [P, DC, 2, NE * DK])
        wa = sb("wa", [P, DC, NE * RANK])
        bm = sb("bm", [NE * RANK, D])
        xt = [sb(f"xt{i}", [P, D]) for i in range(2)]
        xb = [sb(f"xb{i}", [P, D]) for i in range(2)]
        x1 = [sb(f"x1_{i}", [P, D]) for i in range(2)]
        hid = [sb(f"hid{i}", [P, D]) for i in range(2)]
        wcur = [sb(f"wcur{i}", [P, 2, P]) for i in range(2)]
        ypre = sb("ypre", [P, DC, BT, S])
        yT = [sb(f"yT{i}", [P, DC, P]) for i in range(2)]
        kk = sb("kk", [P, NE * DK])
        prod = sb("prod", [P, NE * DK])
        sc = sb("sc", [P, NE])
        negm = sb("negm", [P, 1])
        ex = sb("ex", [P, NE])
        tot = sb("tot", [P, 1])
        rtot = sb("rtot", [P, 1])
        wn = sb("wn", [P, NE])
        wh = sb("wh", [P, NE, RANK])
        whT = sb("whT", [P, P])

        psH = [ps(f"psH{i}", [P, D]) for i in range(2)]
        psY = ps("psY", [P, DC, BT, S])
        psR = ps("psR", [P, D])
        psQK = ps("psQK", [P, 2, NE * DK])
        psA = ps("psA", [P, NE, RANK])
        psT = ps("psT", [P, P])
        psX = ps("psX", [P, DC, P])

        weights_in = sem("l0_weights_in")
        x_in = [sem(f"l0_x_in{i}") for i in range(2)]
        x1_out = [sem(f"l0_x1_out{i}") for i in range(2)]
        wcur_ready = sem("l0_wcur_ready")
        hid_mm = sem("l0_hid_mm")
        hid_ready = sem("l0_hid_ready")
        y_mm = sem("l0_y_mm")
        ypre_ready = sem("l0_ypre_ready")
        yT_ready = sem("l0_yT_ready")
        ffn_mm = sem("l0_ffn_mm")
        kk_ready = sem("l0_kk_ready")
        prod_ready = sem("l0_prod_ready")
        sc_ready = sem("l0_sc_ready")
        negm_ready = sem("l0_negm_ready")
        ex_ready = sem("l0_ex_ready")
        rtot_ready = sem("l0_rtot_ready")
        wn_ready = sem("l0_wn_ready")
        wh_ready = sem("l0_wh_ready")
        whT_mm = sem("l0_whT_mm")
        whT_ready = sem("l0_whT_ready")
        sum_mm = sem("l0_sum_mm")
        xb_ready = sem("l0_xb_ready")
        x1_ready = sem("l0_x1_ready")
        xT_mm = sem("l0_xT_mm")
        hi_ready = sem("l0_hi_ready")
        lo_ready = sem("l0_lo_ready")

        block = ctx.enter_context(nc.Block())

        def tiles(eng, body):
            for u in range(2):
                body(u, u)
            with eng.Fori(1, NT // 2 - 1) as pair:
                for u in range(2):
                    body(pair * 2 + u, u)
            for u in range(2):
                body(NT - 2 + u, u)

        def first(tile):
            return isinstance(tile, int) and tile == 0

        def last(tile):
            return isinstance(tile, int) and tile == NT - 1

        @block.sync
        def _(sp):
            sp.dma_start(xt[0][:], d["x"][0:P, :]).then_inc(x_in[0], 16)
            sp.dma_start(xt[1][:], d["x"][P:2 * P, :]).then_inc(x_in[1], 16)
            sp.dma_start(w0[:], d["w0"]).then_inc(weights_in, 16)
            sp.dma_start(wqk[:, :, 0, :], d["wq0"]).then_inc(weights_in, 16)
            sp.dma_start(wqk[:, :, 1, :], d["wk0"]).then_inc(weights_in, 16)
            sp.dma_start(wa[:], d["wa"]).then_inc(weights_in, 16)
            sp.dma_start(bm[:], d["bm"]).then_inc(weights_in, 16)

            def body(tile, u):
                sp.wait_ge(x1_ready, tile + 1)
                sp.dma_start(d["x1"][bass.ds(tile * P, P), :], x1[u][:]).then_inc(x1_out[u], 16)
                if not (isinstance(tile, int) and tile >= NT - 2):
                    sp.wait_ge(hid_mm, tile + 1)
                    sp.wait_ge(xb_ready, tile + 1)
                    sp.dma_start(xt[u][:], d["x"][bass.ds(tile * P + 2 * P, P), :]).then_inc(x_in[u], 16)

            tiles(sp, body)
            for u in range(2):
                sp.wait_ge(x1_out[u], 16 * (NT // 2))

        @block.gpsimd
        def _(pool):
            def body(tile, u, turn):
                if started(turn):
                    pool.wait_ge(hid_mm, tile - 1)
                nc.gpsimd.tensor_copy(wcur[u][:], t["wsel"][:, bass.ds(tile, 1), :, :]
                                      .rearrange("p a j h -> p (a j) h")).then_inc(wcur_ready, 1)
                pool.wait_ge(x_in[u], 16 * (turn + 1))
                if started(turn):
                    pool.wait_ge(x1_ready, tile - 1)
                nc.gpsimd.tensor_tensor(xb[u][:], xt[u][:], t["bias0"][:], ALU.add).then_inc(xb_ready, 1)

            for u in range(2):
                body(u, u, 0)
            with pool.Fori(1, NT // 2) as pair:
                for u in range(2):
                    body(pair * 2 + u, u, pair)

        @block.tensor
        def _(pe):
            def session(tile, u, turn):
                pe.wait_ge(x_in[u], 16 * (turn + 1))
                pe.wait_ge(wcur_ready, tile + 1)
                if not first(tile):
                    pe.wait_ge(hid_ready, tile)
                for i in range(2):
                    last_mm = pe.matmul(psH[i][:], wcur[u][:, i, :], xt[u][:], start=True, stop=True)
                last_mm.then_inc(hid_mm, 1)
                pe.wait_ge(hid_ready, tile + 1)
                if not first(tile):
                    pe.wait_ge(ypre_ready, tile)
                for c in range(DC):
                    for i in range(2):
                        last_mm = pe.matmul(psY[:, c, 2 * i:2 * i + 2, :], hid[i][:, c * P:(c + 1) * P], t["w2"][:],
                                            start=True, stop=True)
                last_mm.then_inc(y_mm, 1)

            def x1_transposes(tile, u):
                pe.wait_ge(x1_ready, tile + 1)
                if not first(tile):
                    pe.wait_ge(lo_ready, tile)
                for c in range(DC):
                    last_mm = pe.transpose(psX[:, c, :], x1[u][:, c * P:(c + 1) * P], t["ident"][:])
                last_mm.then_inc(xT_mm, 1)

            def body(tile, u, turn):
                pe.wait_ge(yT_ready, tile + 1)
                if not first(tile):
                    pe.wait_ge(x1_ready, tile)
                for c in range(DC):
                    pe.matmul(psQK[:].rearrange("p a n -> p (a n)"), yT[u][:, c, :],
                              wqk[:, c, :, :].rearrange("p a n -> p (a n)"), start=(c == 0), stop=(c == DC - 1))
                for c in range(DC):
                    last_mm = pe.matmul(psA[:].rearrange("p e r -> p (e r)"), yT[u][:, c, :], wa[:, c, :],
                                        start=(c == 0), stop=(c == DC - 1))
                last_mm.then_inc(ffn_mm, 1)
                for c in range(DC):
                    pe.matmul(psR[:], yT[u][:, c, :], w0[:, c, :], start=(c == 0), stop=False)
                if not first(tile):
                    x1_transposes(tile - 1, 1 - u)
                if not last(tile):
                    session(tile + 1, 1 - u, turn + u)
                pe.wait_ge(wh_ready, tile + 1)
                pe.transpose(psT[:], wh[:].rearrange("p e r -> p (e r)"), t["ident"][:]).then_inc(whT_mm, 1)
                pe.wait_ge(whT_ready, tile + 1)
                pe.matmul(psR[:], whT[:], bm[:], start=False, stop=True).then_inc(sum_mm, 1)

            session(0, 0, 0)
            pe.wait_ge(weights_in, 16 * 5)
            for u in range(2):
                body(u, u, 0)
            with pe.Fori(1, NT // 2 - 1) as pair:
                for u in range(2):
                    body(pair * 2 + u, u, pair)
            for u in range(2):
                body(NT - 2 + u, u, NT // 2 - 1)
            x1_transposes(NT - 1, 1)

        @block.scalar
        def _(act):
            def gelu(tile):
                act.wait_ge(hid_mm, tile + 1)
                if not first(tile):
                    act.wait_ge(y_mm, tile)
                for i in range(2):
                    ins = nc.scalar.activation(hid[i][:], psH[i][:], ACT.Gelu,
                                               bias=t["bsel"][:, bass.ds(tile, 1), i:i + 1].rearrange("p a b -> p (a b)"))
                ins.then_inc(hid_ready, 1)

            def high(tile):
                act.wait_ge(xT_mm, tile + 1)
                nc.scalar.activation(t["xThi"][:, :, bass.ds(tile * P, P)], psX[:], ACT.Copy).then_inc(hi_ready, 1)

            def body(tile, u):
                act.wait_ge(ffn_mm, tile + 1)
                nc.scalar.activation(kk[:], psQK[:, 1, :], ACT.Copy, scale=1.0 / math.sqrt(DK)).then_inc(kk_ready, 1)
                if not first(tile):
                    high(tile - 1)
                if not last(tile):
                    gelu(tile + 1)
                act.wait_ge(negm_ready, tile + 1)
                nc.scalar.activation(ex[:], sc[:], ACT.Exp, bias=negm[:, 0:1], accum_out=tot[:, 0:1]).then_inc(ex_ready, 1)
                act.wait_ge(whT_mm, tile + 1)
                nc.scalar.activation(whT[:], psT[:], ACT.Copy).then_inc(whT_ready, 1)

            gelu(0)
            tiles(act, body)
            high(NT - 1)

        @block.vector
        def _(dve):
            def sources(tile, u):
                dve.wait_ge(y_mm, tile + 1)
                nc.vector.tensor_tensor(ypre[:], psY[:],
                                        t["b2"][:].unsqueeze(1).unsqueeze(1).to_broadcast([P, DC, BT, S]),
                                        ALU.add).then_inc(ypre_ready, 1)
                dve.wait_ge(ypre_ready, tile + 1)
                if not (isinstance(tile, int) and tile < 2):
                    dve.wait_ge(sum_mm, tile - 1)
                nc.vector.tensor_tensor(yT[u][:].rearrange("p c (b s) -> p c b s", s=S), ypre[:],
                                        t["tmask"][:, :, bass.ds(tile * BT, BT)].unsqueeze(3)
                                        .to_broadcast([P, DC, BT, S]), ALU.mult).then_inc(yT_ready, 1)

            def low(tile):
                dve.wait_ge(hi_ready, tile + 1)
                nc.vector.tensor_tensor(t["xTlo"][:, :, bass.ds(tile * P, P)], psX[:],
                                        t["xThi"][:, :, bass.ds(tile * P, P)].bitcast(F32),
                                        ALU.subtract).then_inc(lo_ready, 1)

            def body(tile, u, turn):
                dve.wait_ge(kk_ready, tile + 1)
                nc.vector.tensor_tensor(prod[:], psQK[:, 0, :], kk[:], ALU.mult).then_inc(prod_ready, 1)
                dve.wait_ge(prod_ready, tile + 1)
                nc.vector.reduce_sum(sc[:], prod[:].rearrange("p (e k) -> p e k", k=DK), AX.X).then_inc(sc_ready, 1)
                dve.wait_ge(sc_ready, tile + 1)
                nc.vector.tensor_reduce(negm[:], sc[:], AX.X, ALU.max, negate=True).then_inc(negm_ready, 1)
                if not first(tile):
                    low(tile - 1)
                dve.wait_ge(ex_ready, tile + 1)
                nc.vector.reciprocal(rtot[:], tot[:]).then_inc(rtot_ready, 1)
                dve.wait_ge(rtot_ready, tile + 1)
                nc.vector.tensor_scalar(wn[:], ex[:], rtot[:, 0:1], None, ALU.mult).then_inc(wn_ready, 1)
                dve.wait_ge(wn_ready, tile + 1)
                nc.vector.tensor_tensor(wh[:], psA[:], wn[:].unsqueeze(2).to_broadcast([P, NE, RANK]),
                                        ALU.mult).then_inc(wh_ready, 1)
                if not last(tile):
                    sources(tile + 1, 1 - u)
                dve.wait_ge(sum_mm, tile + 1)
                dve.wait_ge(xb_ready, tile + 1)
                if started(turn):
                    dve.wait_ge(x1_out[u], 16 * turn)
                    dve.wait_ge(xT_mm, tile - 1)
                nc.vector.tensor_tensor(x1[u][:], psR[:], xb[u][:], ALU.add).then_inc(x1_ready, 1)

            sources(0, 0)
            for u in range(2):
                body(u, u, 0)
            with dve.Fori(1, NT // 2 - 1) as pair:
                for u in range(2):
                    body(pair * 2 + u, u, pair)
            for u in range(2):
                body(NT - 2 + u, u, NT // 2 - 1)
            low(NT - 1)


def projections(nc, t, d):
    NQ, NKC = HQ * HD // D, HK * HD // D
    NG = NQ + 2 * NKC
    U = 4
    with ExitStack() as ctx:
        def sb(name, shape, dt=F32):
            return ctx.enter_context(nc.sbuf_tensor(name, shape, dt))

        def ps(name, shape):
            return ctx.enter_context(nc.psum_tensor(name, shape, F32))

        def sem(name):
            return ctx.enter_context(nc.semaphore(name))

        wraw = [sb(f"wraw{i}", [P, DC, D]) for i in range(2)]
        whi = [sb(f"whi{i}", [P, DC, D], F32R) for i in range(2)]
        wlo = [sb(f"wlo{i}", [P, DC, D], F32R) for i in range(2)]
        squares = sb("squares", [P, G4, HD])
        eps = sb("eps", [P, 1])
        ssq = sb("ssq", [P, U, G4])
        std = sb("std", [P, U, G4])
        rstd = sb("rstd", [P, U, G4])
        straight = [sb(f"straight{i}", [P, G4, HD]) for i in range(2)]
        crossed = [sb(f"crossed{i}", [P, G4, HD]) for i in range(2)]
        turned = [sb(f"turned{i}", [P, G4, HD]) for i in range(U)]
        stage = [sb(f"stage{i}", [P, BT, G4, S]) for i in range(2)]
        psP = [ps(f"psP{i}", [P, G4, HD]) for i in range(U)]
        psTr = [ps(f"psTr{i}", [P, G4, BT, S]) for i in range(2)]

        w_in = [sem(f"p_w_in{i}") for i in range(2)]
        whi_ready = sem("p_whi_ready")
        wlo_ready = sem("p_wlo_ready")
        eps_ready = sem("p_eps_ready")
        proj_mm = sem("p_proj_mm")
        ssq_ready = sem("p_ssq_ready")
        std_ready = sem("p_std_ready")
        rstd_ready = sem("p_rstd_ready")
        parts_ready = sem("p_parts_ready")
        sum_ready = sem("p_sum_ready")
        turned_ready = sem("p_turned_ready")
        heads_mm = sem("p_heads_mm")
        stage_ready = sem("p_stage_ready")
        stored = [sem(f"p_stored{i}") for i in range(2)]

        block = ctx.enter_context(nc.Block())
        NN = (NQ + NKC) * NT

        def is_first(n, count):
            return isinstance(n, int) and n < count

        @block.sync
        def _(sp):
            def load(g, w):
                sp.dma_start(wraw[w][:], d["wqkv"][bass.ds(g, 1), :, :, :].rearrange("a p c n -> (a p) c n"))\
                    .then_inc(w_in[w], 16)

            def chunk(g, w, store):
                if not (isinstance(g, int) and g >= NG - 2):
                    sp.wait_ge(wlo_ready, g + 1)
                    load(g + 2, w)
                with sp.Fori(0, NT // 2) as pair:
                    for u in range(2):
                        sp.wait_ge(stage_ready, g * NT + pair * 2 + u + 1)
                        store(g, pair * 2 + u, u)

            def queries(g, tile, u):
                dst = d["qT"].rearrange("(t j) p (g n) -> t g p j n", j=BT, g=NQ)
                sp.dma_start(dst[bass.ds(tile, 1), bass.ds(g, 1), :, :, :].rearrange("a b p j n -> (a b p) j n"),
                             stage[u][:].rearrange("p j h s -> p j (h s)")).then_inc(stored[u], 16)

            def keys(g, tile, u):
                dst = d["kTn"].rearrange("(t j) p (g n) -> t g p j n", j=BT, g=NKC)
                sp.dma_start(dst[bass.ds(tile, 1), bass.ds(g - NQ, 1), :, :, :].rearrange("a b p j n -> (a b p) j n"),
                             stage[u][:].rearrange("p j h s -> p j (h s)")).then_inc(stored[u], 16)

            def values(g, tile, u):
                sp.dma_start(d["vn"][bass.ds(tile * P, P), (g - NQ - NKC) * D:(g - NQ - NKC + 1) * D],
                             stage[u][:].rearrange("p j h s -> p (j h s)")).then_inc(stored[u], 16)

            load(0, 0)
            load(1, 1)
            with sp.Fori(0, NQ // 2) as pair:
                for w in range(2):
                    chunk(pair * 2 + w, w, queries)
            for w in range(2):
                chunk(NQ + w, w, keys)
            for w in range(2):
                chunk(NQ + NKC + w, w, values)
            for u in range(2):
                sp.wait_ge(stored[u], 16 * NG * NT // 2)

        @block.gpsimd
        def _(pool):
            nc.gpsimd.memset(eps[:], EPS).then_inc(eps_ready, 1)

            def body(turn, u):
                n = turn * U + u
                pool.wait_ge(parts_ready, n + 1)
                nc.gpsimd.tensor_tensor(straight[u % 2][:], straight[u % 2][:], crossed[u % 2][:], ALU.add)\
                    .then_inc(sum_ready, 1)
                if started(turn):
                    pool.wait_ge(heads_mm, n - 3)
                pool.wait_ge(sum_ready, n + 1)
                nc.gpsimd.tensor_tensor(turned[u][:], straight[u % 2][:],
                                        rstd[:, u, :].unsqueeze(2).to_broadcast([P, G4, HD]), ALU.mult)\
                    .then_inc(turned_ready, 1)

            for u in range(U):
                body(0, u)
            with pool.Fori(1, NN // U) as turn:
                for u in range(U):
                    body(turn, u)

        @block.tensor
        def _(pe):
            def transposes(m, i):
                pe.wait_ge(turned_ready, m + 1)
                if not is_first(m, 2):
                    pe.wait_ge(stage_ready, m - 1)
                for h in range(G4):
                    mm = pe.transpose(psTr[i % 2][:, h, :, :].rearrange("p j s -> p (j s)"),
                                      turned[i % U][:, h, :], t["ident"][:])
                mm.then_inc(heads_mm, 1)

            def chunk(g, w, heads):
                pe.wait_ge(wlo_ready, g + 1)
                for tile in range(NT):
                    n = g * NT + tile
                    if heads and not is_first(n, U):
                        pe.wait_ge(parts_ready, n - 3)
                    if not heads:
                        pe.wait_ge(stage_ready, n - 3)
                    cols = slice(tile * P, (tile + 1) * P)
                    for c in range(DC):
                        mm = split3(pe, psP[tile % U][:].rearrange("p h n -> p (h n)"),
                                    (t["xThi"][:, c, cols], t["xTlo"][:, c, cols]),
                                    (whi[w][:, c, :], wlo[w][:, c, :]), c == 0, c == DC - 1)
                    mm.then_inc(proj_mm, 1)
                    if heads and not is_first(n, 2):
                        transposes(n - 2, tile + 2)

            for w in range(2):
                chunk(w, w, True)
            with pe.Fori(1, (NQ + NKC) // 2) as pair:
                for w in range(2):
                    chunk(pair * 2 + w, w, True)
            for i in range(2):
                transposes(NN - 2 + i, U - 2 + i)
            for w in range(2):
                chunk(NQ + NKC + w, w, False)

        @block.scalar
        def _(act):
            def weights(g, w, turn):
                act.wait_ge(w_in[w], 16 * (turn + 1))
                if started(turn):
                    act.wait_ge(proj_mm, (g - 1) * NT)
                nc.scalar.activation(whi[w][:], wraw[w][:], ACT.Copy).then_inc(whi_ready, 1)

            def norms(turn, u):
                n = turn * U + u
                act.wait_ge(proj_mm, n + 1)
                for h in range(G4):
                    ins = nc.scalar.activation(squares[:, h, :], psP[u][:, h, :], ACT.Square,
                                               accum_out=ssq[:, u, h:h + 1])
                ins.then_inc(ssq_ready, 1)
                act.wait_ge(ssq_ready, n + 1)
                nc.scalar.activation(std[:, u, :], ssq[:, u, :], ACT.Sqrt, bias=eps[:, 0:1], scale=1.0 / HD)\
                    .then_inc(std_ready, 1)

            def copy_out(turn, u):
                m = turn * U + u - 2
                act.wait_ge(heads_mm, m + 1)
                if not is_first(m, 2):
                    act.wait_ge(stored[u % 2], 16 * (2 * turn + (u - 2) // 2))
                nc.scalar.activation(stage[u % 2][:].rearrange("p j h s -> p h j s"), psTr[u % 2][:], ACT.Copy)\
                    .then_inc(stage_ready, 1)

            def chunk(g, w, turn0, peel):
                weights(g + 1, 1 - w, turn0 + w)
                if peel:
                    for u in range(U):
                        norms(0, u)
                        if u >= 2:
                            copy_out(0, u)
                with act.Fori(1 if peel else 0, NT // U) as k:
                    for u in range(U):
                        norms(g * (NT // U) + k, u)
                        copy_out(g * (NT // U) + k, u)

            act.wait_ge(eps_ready, 1)
            weights(0, 0, 0)
            chunk(0, 0, 0, True)
            chunk(1, 1, 0, False)
            with act.Fori(1, (NQ + NKC) // 2) as pair:
                for w in range(2):
                    chunk(pair * 2 + w, w, pair, False)
            for u in range(2):
                copy_out(NN // U, u)
            weights(NG - 1, 1, NG // 2 - 1)
            with act.Fori(NN // U, NG * NT // U) as turn:
                for u in range(U):
                    n = turn * U + u
                    act.wait_ge(proj_mm, n + 1)
                    act.wait_ge(stored[u % 2], 16 * (2 * turn + u // 2))
                    nc.scalar.activation(stage[u % 2][:].rearrange("p j h s -> p (j h s)"),
                                         psP[u][:].rearrange("p h n -> p (h n)"), ACT.Copy)\
                        .then_inc(stage_ready, 1)

        @block.vector
        def _(dve):
            def weights(g, w):
                dve.wait_ge(whi_ready, g + 1)
                nc.vector.tensor_tensor(wlo[w][:], wraw[w][:], whi[w][:].bitcast(F32), ALU.subtract)\
                    .then_inc(wlo_ready, 1)

            def norms(turn, u, tile, cos, sin):
                n = turn * U + u
                half = HD // 2
                dve.wait_ge(std_ready, n + 1)
                nc.vector.reciprocal(rstd[:, u, :], std[:, u, :]).then_inc(rstd_ready, 1)
                if not is_first(n, 2):
                    dve.wait_ge(turned_ready, n - 1)
                c = cos[:, bass.ds(tile, 1), :].to_broadcast([P, G4, HD])
                s = sin[:, bass.ds(tile, 1), :].to_broadcast([P, G4, HD])
                nc.vector.tensor_tensor(straight[u % 2][:], psP[u][:], c, ALU.mult)
                nc.vector.tensor_tensor(crossed[u % 2][:, :, 0:half], psP[u][:, :, half:HD], s[:, :, 0:half], ALU.mult)
                nc.vector.tensor_tensor(crossed[u % 2][:, :, half:HD], psP[u][:, :, 0:half], s[:, :, half:HD], ALU.mult)\
                    .then_inc(parts_ready, 1)

            def chunk(g, w, cos, sin, peel=False):
                weights(g + 1, 1 - w)
                if peel:
                    for u in range(U):
                        norms(0, u, u, cos, sin)
                with dve.Fori(1 if peel else 0, NT // U) as k:
                    for u in range(U):
                        norms(g * (NT // U) + k, u, k * U + u, cos, sin)

            weights(0, 0)
            chunk(0, 0, t["cosq"], t["sinq"], True)
            chunk(1, 1, t["cosq"], t["sinq"])
            with dve.Fori(1, NQ // 2) as pair:
                for w in range(2):
                    chunk(pair * 2 + w, w, t["cosq"], t["sinq"])
            for w in range(2):
                chunk(NQ + w, w, t["cosk"], t["sink"])
            weights(NG - 1, 1)


def attention(nc, t, d):
    ROWS = REP * S
    NH = HK
    STEPS = BT * NH
    NG = NT
    SPLIT = NH
    AHEAD = 5
    TURNED = 2
    NPB = NPP + 1
    CH = L // P
    QUADS = STEPS // G4
    W = L + S
    HW = W // 2
    with ExitStack() as ctx:
        def sb(name, shape, dt=F32):
            return ctx.enter_context(nc.sbuf_tensor(name, shape, dt))

        def ps(name, shape):
            return ctx.enter_context(nc.psum_tensor(name, shape, F32))

        def sem(name):
            return ctx.enter_context(nc.semaphore(name))

        kst = [sb(f"kst{i}", [P, NPB, HK, PSIZE]) for i in range(2)]
        khi = sb("khi", [P, HK, W], F32R)
        klo = sb("klo", [P, HK, W], F32R)
        vst = [sb(f"vst{i}", [P, CH, HK * HD]) for i in range(2)]
        qst = [sb(f"qst{i}", [P, HK * ROWS]) for i in range(2)]
        qhi = [sb(f"qhi{i}", [P, HK * ROWS], F32R) for i in range(2)]
        qlo = [sb(f"qlo{i}", [P, HK * ROWS], F32R) for i in range(2)]
        vnew = sb("vnew", [P, HK // G4, G4, HD])
        rows = [sb(f"rows{i}", [P, CH], I32) for i in range(2)]
        mask = [sb(f"mask{i}", [P, W]) for i in range(2)]
        negm = sb("negm3", [P, NH])
        tot = sb("tot3", [P, NH])
        rtot = sb("rtot3", [P, NH])
        p_sb = sb("p_sb", [P, NH, W])
        pn_sb = sb("pn_sb", [P, NH, S])
        pT = [sb(f"pT{i}", [P, L]) for i in range(4)]
        pTn = [sb(f"pTn{i}", [P, ROWS]) for i in range(2)]
        oT = [sb(f"oT{i}", [P, G4 * ROWS]) for i in range(2)]

        psS = [ps(f"psS{i}", [P, 2, 512]) for i in range(2)]
        psN = psS[1][:, 0, HW:HW + ROWS]
        psT = [ps(f"psTp{i}", [P, L]) for i in range(2)]
        psO = [ps(f"psO{i}", [P, G4, ROWS]) for i in range(2)]

        k_in = [sem(f"a_k_in{i}") for i in range(2)]
        q_in = [sem(f"a_q_in{i}") for i in range(2)]
        v_in = [sem(f"a_v_in{i}") for i in range(2)]
        vnew_in = sem("a_vnew_in")
        zeroed = sem("a_zeroed")
        rows_ready = sem("a_rows_ready")
        khi_ready = sem("a_khi_ready")
        klo_ready = sem("a_klo_ready")
        qhi_ready = sem("a_qhi_ready")
        qlo_ready = sem("a_qlo_ready")
        mask_ready = sem("a_mask_ready")
        s_mm = sem("a_s_mm")
        s_ready = sem("a_s_ready")
        e_ready = sem("a_e_ready")
        r_ready = sem("a_r_ready")
        p_ready = sem("a_p_ready")
        pT_mm = sem("a_pT_mm")
        pT_ready = sem("a_pT_ready")
        pTn_mm = sem("a_pTn_mm")
        pTn_ready = sem("a_pTn_ready")
        pv_mm = sem("a_pv_mm")
        oT_ready = sem("a_oT_ready")
        oT_out = [sem(f"a_oT_out{i}") for i in range(2)]

        block = ctx.enter_context(nc.Block())

        def zero(x, n=1):
            return isinstance(x, int) and x < n

        def groups(eng, body):
            body(0, False)
            with eng.Fori(1, NG - 1) as g:
                body(g, False)
            body(NG - 1, True)

        @block.sync
        def _(sp):
            pages = [sp.alloc_register(f"page{k}") for k in range(NPP)]
            used = sp.alloc_register("used")
            sp.reg_mov(used, 0)

            def batch(g, j, early=False):
                b, i = g * BT + j, j % 2
                if not early:
                    sp.reg_add(used, used, NH)
                    sp.wait_ge(zeroed, 1)
                    sp.wait_ge(klo_ready, used)
                sp.load(pages, d["table"].rearrange("(o n) -> o n", o=1)[:, bass.ds(b * NPP, NPP)])
                for k in range(NPP):
                    page = sp.snap(pages[k], min_val=0, max_val=PAGES - 1)
                    sp.dma_start(kst[i][:, k, :, :].rearrange("p h n -> p (h n)"),
                                 d["kT"][bass.ds(page, 1), :, :].rearrange("a p n -> (a p) n")).then_inc(k_in[i], 16)
                sp.dma_start(kst[i][:, NPP, :, :].rearrange("p h n -> p (h n)"),
                             d["kTn"][bass.ds(b, 1), :, :].rearrange("a p n -> (a p) n")).then_inc(k_in[i], 16)
                if not early:
                    sp.wait_ge(qlo_ready, b - 1)
                sp.dma_start(qst[i][:], d["qT"][bass.ds(b, 1), :, :].rearrange("a p n -> (a p) n")).then_inc(q_in[i], 16)

            def new_values(g, j):
                b = g * BT + j
                if not zero(b):
                    sp.wait_ge(pv_mm, b * NH)
                src = d["vn"].rearrange("(b s) (q h n) -> h b s q n", s=S, q=HK // G4, h=G4)
                for h in range(G4):
                    sp.dma_start(vnew[h * S:(h + 1) * S, :, h, :],
                                 src[h, bass.ds(b, 1), :, :, :].rearrange("a s q n -> (a s) q n")).then_inc(vnew_in, 16)

            batch(0, 0, True)
            batch(0, 1, True)
            sp.wait_ge(zeroed, 1)
            new_values(0, 0)
            batch(0, 2)
            new_values(0, 1)
            batch(0, 3)
            new_values(0, 2)
            with sp.Fori(1, NG) as g:
                for j in range(BT):
                    batch(g, j)
                    new_values(g, j - 1)
            new_values(NG, -1)

        @block.gpsimd
        def _(pool):
            nc.gpsimd.memset(vnew[:], 0.0).then_inc(zeroed, 1)
            copied = pool.alloc_register("copied")
            pool.reg_mov(copied, 0)

            def values(g, j, early=False):
                b, i = g * BT + j, j % 2
                if not early:
                    pool.wait_ge(pv_mm, b * NH - NH)
                nc.gpsimd.tensor_copy(rows[i][:], t["vrows"][:, bass.ds(b, 1), :].rearrange("p a c -> p (a c)"))\
                    .then_inc(rows_ready, 1)
                pool.reg_add(copied, copied, 1)
                pool.wait_ge(zeroed, 1)
                pool.wait_ge(rows_ready, copied)
                gather(i, 0)

            def gather(i, c):
                nc.gpsimd.indirect_dma_start(vst[i][:, c, :], None, d["v"],
                                             bass.IndirectOffsetOnAxis(rows[i][:, c:c + 1], 0)).then_inc(v_in[i], 16)

            def low(g, l):
                m, i, h = g * STEPS + l, l // NH % 2, l % NH
                pool.wait_ge(khi_ready, m + 1)
                nc.gpsimd.tensor_tensor(klo[:, h, :].rearrange("p (k n) -> p k n", n=PSIZE), kst[i][:, :, h, :],
                                        khi[:, h, :].rearrange("p (k n) -> p k n", n=PSIZE).bitcast(F32), ALU.subtract)\
                    .then_inc(klo_ready, 1)

            values(0, 0, True)
            for c in range(1, CH):
                gather(0, c)
            for l in range(SPLIT):
                low(0, l)
            values(0, 1, True)
            for c in range(1, CH):
                gather(1, c)

            def group(g, last):
                for l in range(STEPS):
                    if l + SPLIT < STEPS or not last:
                        low(g, l + SPLIT)
                    if (l // NH + 1 < BT or not last) and not zero(g * STEPS + l, NH):
                        if l % NH == 0:
                            values(g, l // NH + 1)
                        elif l % NH < CH:
                            gather((l // NH + 1) % 2, l % NH)

            groups(pool, group)

        @block.tensor
        def _(pe):
            def scores(g, l):
                m, i, h = g * STEPS + l, l // NH % 2, l % NH
                if not zero(m, 2):
                    pe.wait_ge(s_ready, m - 1)
                if l % G4 == G4 - 1 and not zero(m, G4):
                    pe.wait_ge(pTn_ready, g * QUADS + l // G4)
                if h == 0:
                    pe.wait_ge(qlo_ready, g * BT + l // NH + 1)
                pe.wait_ge(klo_ready, m + 1)
                qs = slice(h * ROWS, (h + 1) * ROWS)
                for k in range(2):
                    ks = slice(k * HW, (k + 1) * HW)
                    mm = split3(pe, psS[l % 2][:, k, 0:HW], (qhi[i][:, qs], qlo[i][:, qs]),
                                (khi[:, h, ks], klo[:, h, ks]), True, True)
                mm.then_inc(s_mm, 1)

            def transposes(g, l, last=False):
                m = g * STEPS + l
                pe.wait_ge(p_ready, m + 1)
                if not zero(m, 2):
                    pe.wait_ge(pT_ready, m - 1)
                for c in range(CH):
                    mm = pe.transpose(psT[l % 2][:, c * P:(c + 1) * P], p_sb[:, l % NH, c * P:(c + 1) * P], t["ident"][:])
                mm.then_inc(pT_mm, 1)
                if l % G4 == G4 - 1:
                    pe.wait_ge(s_ready, m + 1 if last and l == STEPS - 1 else m + 3)
                    first = l % NH - G4 + 1
                    pe.transpose(psN, pn_sb[:, first:first + G4, :].rearrange("p h s -> p (h s)"),
                                 t["ident"][:]).then_inc(pTn_mm, 1)

            def products(g, l):
                m, i, h = g * STEPS + l, l // NH % 2, l % NH
                quad = g * QUADS + l // G4
                turn = g * (BT // 2) + l // NH // 2 + 1
                out = psO[l // G4 % 2]
                if h == 0:
                    pe.wait_ge(v_in[i], 16 * CH * turn)
                if l % G4 == 0 and not zero(quad, 2):
                    pe.wait_ge(oT_ready, quad - 1)
                pe.wait_ge(pT_ready, m + 1)
                for c in range(CH):
                    mm = pe.matmul(out[:, l % G4, :], vst[i][:, c, h * HD:(h + 1) * HD], pT[l % 4][:, c * P:(c + 1) * P],
                                   start=(l % G4 == 0 and c == 0), stop=False, skip_group_check=True)
                if l % G4 == G4 - 1:
                    pe.wait_ge(pTn_ready, quad + 1)
                    if h == G4 - 1:
                        pe.wait_ge(vnew_in, 16 * G4 * (g * BT + l // NH + 1))
                    for k in range(G4):
                        mm = pe.matmul(out[:, k, :], vnew[:, h // G4, k, :], pTn[l // G4 % 2][:],
                                       start=False, stop=(k == G4 - 1), skip_group_check=True)
                mm.then_inc(pv_mm, 1)

            for l in range(AHEAD):
                scores(0, l)
            for l in range(TURNED):
                transposes(0, l)

            def group(g, last):
                for l in range(STEPS):
                    if l + AHEAD < STEPS or not last:
                        scores(g, l + AHEAD)
                    if l + TURNED < STEPS or not last:
                        transposes(g, l + TURNED, last)
                    products(g, l)

            groups(pe, group)

        @block.scalar
        def _(act):
            def queries(g, j):
                b, i = g * BT + j, j % 2
                act.wait_ge(q_in[i], 16 * (g * (BT // 2) + j // 2 + 1))
                if not zero(b, 2):
                    act.wait_ge(s_mm, b * NH - NH)
                nc.scalar.activation(qhi[i][:], qst[i][:], ACT.Copy).then_inc(qhi_ready, 1)

            def high(g, l):
                m, i, h = g * STEPS + l, l // NH % 2, l % NH
                if h == 0:
                    act.wait_ge(k_in[i], 16 * NPB * (g * (BT // 2) + l // NH // 2 + 1))
                if not zero(m, NH):
                    act.wait_ge(s_mm, m - NH + 1)
                nc.scalar.activation(khi[:, h, :].rearrange("p (k n) -> p k n", n=PSIZE), kst[i][:, :, h, :], ACT.Copy)\
                    .then_inc(khi_ready, 1)

            def exps(g, l):
                m, h = g * STEPS + l, l % NH
                act.wait_ge(s_ready, m + 1)
                nc.scalar.activation(p_sb[:, h, :], p_sb[:, h, :], ACT.Exp, bias=negm[:, h:h + 1], scale=-1.0,
                                     accum_out=tot[:, h:h + 1]).then_inc(e_ready, 1)

            def probs_out(g, l):
                m = g * STEPS + l
                act.wait_ge(pT_mm, m + 1)
                if not zero(m, 4):
                    act.wait_ge(pv_mm, m - 3)
                nc.scalar.activation(pT[l % 4][:], psT[l % 2][:], ACT.Copy).then_inc(pT_ready, 1)
                if l % G4 == G4 - 1:
                    quad = g * QUADS + l // G4
                    act.wait_ge(pTn_mm, quad + 1)
                    if not zero(quad, 2):
                        act.wait_ge(pv_mm, (quad - 1) * G4)
                    nc.scalar.activation(pTn[l // G4 % 2][:], psN, ACT.Copy).then_inc(pTn_ready, 1)

            queries(0, 0)
            for l in range(SPLIT):
                high(0, l)
            for l in range(AHEAD - 1):
                exps(0, l)
                if l == AHEAD - 2:
                    for k in range(TURNED):
                        probs_out(0, k)

            def group(g, last):
                for l in range(STEPS):
                    if l + AHEAD - 1 < STEPS or not last:
                        exps(g, l + AHEAD - 1)
                    if l + SPLIT < STEPS or not last:
                        high(g, l + SPLIT)
                    if l + TURNED < STEPS or not last:
                        probs_out(g, l + TURNED)
                    if l % NH == 1 and (l // NH + 1 < BT or not last):
                        queries(g, l // NH + 1)
                    if l % G4 == 1 and not zero(g * STEPS + l, G4):
                        send(g, l // G4 - 1)

            def send(g, q):
                quad = g * QUADS + q
                i = q % 2
                act.wait_ge(oT_ready, quad + 1)
                dst = d["oT"].rearrange("(t j) p (q n) -> t p j q n", j=BT, q=2)
                tile = g + q // QUADS
                act.dma_start(dst[bass.ds(tile, 1), :, q // 2 % BT, i, :].rearrange("a p n -> (a p) n"), oT[i][:])\
                    .then_inc(oT_out[i], 16)

            groups(act, group)
            send(NG - 1, QUADS - 1)
            for i in range(2):
                act.wait_ge(oT_out[i], 16 * NG * QUADS // 2)

        @block.vector
        def _(dve):
            def queries(g, j):
                b, i = g * BT + j, j % 2
                dve.wait_ge(qhi_ready, b + 1)
                nc.vector.tensor_tensor(qlo[i][:], qst[i][:], qhi[i][:].bitcast(F32), ALU.subtract).then_inc(qlo_ready, 1)
                if not zero(b, 2):
                    dve.wait_ge(s_ready, b * NH - NH)
                nc.vector.tensor_scalar(mask[i][:, 0:L], t["key_no"][:],
                                        t["cached"][:, bass.ds(b, 1)], MASKED, ALU.is_ge, ALU.mult).then_inc(mask_ready, 1)

            def scores_done(g, l):
                m, h = g * STEPS + l, l % NH
                if h == 0:
                    dve.wait_ge(mask_ready, g * BT + l // NH + 2)
                if not zero(m, NH):
                    dve.wait_ge(pTn_mm, g * QUADS + l // G4 - 1)
                dve.wait_ge(s_mm, m + 1)

            def least(g, l):
                i, h = l // NH % 2, l % NH
                nc.vector.tensor_tensor_reduce(out=p_sb[:, h, :].rearrange("p (k n) -> p k n", k=2),
                                               in0=psS[l % 2][:, :, 0:HW],
                                               in1=mask[i][:].rearrange("p (k n) -> p k n", k=2), scale=-SCALE,
                                               scalar=BIG, op0=ALU.add, op1=ALU.min,
                                               accum_out=negm[:, h:h + 1]).then_inc(s_ready, 1)

            def norm(g, l):
                m, h = g * STEPS + l, l % NH
                dve.wait_ge(e_ready, m + 1)
                nc.vector.reciprocal(rtot[:, h:h + 1], tot[:, h:h + 1]).then_inc(r_ready, 1)
                dve.wait_ge(r_ready, m + 1)
                nc.vector.tensor_scalar(p_sb[:, h, 0:L], p_sb[:, h, 0:L], rtot[:, h:h + 1], None, ALU.mult)

            def norm_new(g, l):
                h = l % NH
                nc.vector.tensor_scalar(pn_sb[:, h, :], p_sb[:, h, L:W], rtot[:, h:h + 1], None, ALU.mult)\
                    .then_inc(p_ready, 1)

            def output(g, q):
                quad = g * QUADS + q
                dve.wait_ge(pv_mm, (quad + 1) * G4)
                if not zero(quad, 2):
                    dve.wait_ge(oT_out[q % 2], 16 * (g * (QUADS // 2) + q // 2))
                nc.vector.tensor_copy(oT[q % 2][:], psO[q % 2][:].rearrange("p k r -> p (k r)")).then_inc(oT_ready, 1)

            nc.vector.memset(mask[0][:, L:W], 0.0)
            nc.vector.memset(mask[1][:, L:W], 0.0).then_inc(mask_ready, 1)
            queries(0, 0)
            for l in range(AHEAD):
                if l > 1:
                    norm(0, l - 2)
                    norm_new(0, l - 2)
                scores_done(0, l)
                least(0, l)

            def group(g, last):
                for l in range(STEPS):
                    ahead = l + AHEAD < STEPS or not last
                    if l + AHEAD - 2 < STEPS or not last:
                        norm(g, l + AHEAD - 2)
                        if ahead:
                            scores_done(g, l + AHEAD)
                        norm_new(g, l + AHEAD - 2)
                    if ahead:
                        least(g, l + AHEAD)
                    if l % G4 == 0 and not zero(g * STEPS + l):
                        output(g, l // G4 - 1)
                    if l % NH == 1 and (l // NH + 1 < BT or not last):
                        queries(g, l // NH + 1)

            groups(dve, group)
            output(NG - 1, QUADS - 1)


def output_ffn(nc, t, d):
    PARTS = 4
    HP = HQ // PARTS
    HR = HQ // 2
    WR = 4
    with ExitStack() as ctx:
        def sb(name, shape, dt=F32):
            return ctx.enter_context(nc.sbuf_tensor(name, shape, dt))

        def ps(name, shape):
            return ctx.enter_context(nc.psum_tensor(name, shape, F32))

        def sem(name):
            return ctx.enter_context(nc.semaphore(name))

        wohi = sb("wohi", [P, HQ, D], F32R)
        wolo = sb("wolo", [P, HQ, D], F32R)
        raw = [sb(f"raw{i}", [P, WR * D]) for i in range(2)]
        oThi = sb("oThi", [P, HQ, P], F32R)
        oTlo = sb("oTlo", [P, HQ, P], F32R)
        wb = sb("wb", [P, DC, D], F32R)
        gate = sb("gate", [P, DC, NE])
        in_sc = sb("in_sc", [NE, D])
        out_sc = sb("out_sc", [NE, D])
        bias1 = sb("bias1", [P, D])
        att = sb("att", [P, D])
        attT = sb("attT", [P, DC * P])
        zhi = sb("zhi", [P, DC * P], F32R)
        zlo = sb("zlo", [P, DC * P], F32R)
        rneg = sb("rneg", [P, 1])
        rex = sb("rex", [P, NE])
        rsum = sb("rsum", [P, 1])
        rrec = sb("rrec", [P, 1])
        route = sb("route", [P, NE])
        routeT = sb("routeT", [NE, P])
        x1b = sb("x1b", [P, D])

        psW = [ps(f"psW{i}", [P, D]) for i in range(2)]
        psF = ps("psF", [P, D])
        psZ = ps("psZ", [P, D])

        weights_in = sem("o_weights_in")
        raw_in = [sem(f"o_raw_in{i}") for i in range(2)]
        wo_high = sem("o_wo_high")
        wo_low = sem("o_wo_low")
        wb_in = sem("o_wb_in")
        sign_ready = sem("o_sign_ready")
        oT_high = sem("o_oT_high")
        oT_low = sem("o_oT_low")
        wo_mm = sem("o_wo_mm")
        att_ready = sem("o_att_ready")
        attT_mm = sem("o_attT_mm")
        attT_ready = sem("o_attT_ready")
        logit_mm = sem("o_logit_mm")
        rneg_ready = sem("o_rneg_ready")
        rex_ready = sem("o_rex_ready")
        rrec_ready = sem("o_rrec_ready")
        route_ready = sem("o_route_ready")
        routeT_mm = sem("o_routeT_mm")
        routeT_ready = sem("o_routeT_ready")
        in_mm = sem("o_in_mm")
        z_ready = sem("o_z_ready")
        zhi_ready = sem("o_zhi_ready")
        zlo_ready = sem("o_zlo_ready")
        out_mm = sem("o_out_mm")
        osc_ready = sem("o_osc_ready")
        ffn_mm = sem("o_ffn_mm")
        scaled = sem("o_scaled")
        biased = sem("o_biased")
        fin_ready = sem("o_fin_ready")
        x1_in = sem("o_x1_in")
        fin_out = sem("o_fin_out")

        block = ctx.enter_context(nc.Block())
        NW = HQ // WR
        RAW0 = 16 * NW // 2

        def zero(x, n=1):
            return isinstance(x, int) and x < n

        def tiles(eng, body):
            body(0, 0)
            body(1, 1)
            with eng.Fori(1, NT // 2) as pair:
                for u in range(2):
                    body(pair * 2 + u, u)

        @block.sync
        def _(sp):
            def raw_heads(tile, i):
                src = d["oT"].rearrange("(t j) p (q n) -> t q p j n", j=BT, q=2)
                sp.dma_start(raw[i][:].rearrange("p (j n) -> p j n", j=BT),
                             src[bass.ds(tile, 1), i, :, :, :].rearrange("a p j n -> (a p) j n")).then_inc(raw_in[i], 16)

            for k in range(NW):
                if k >= 2:
                    sp.wait_ge(wo_low, k - 1)
                sp.dma_start(raw[k % 2][:].rearrange("p (h n) -> p h n", n=D), d["wo"][:, k * WR:(k + 1) * WR, :])\
                    .then_inc(raw_in[k % 2], 16)
                if k == 1:
                    sp.dma_start(gate[:], d["gate"]).then_inc(weights_in, 16)
                    sp.dma_start(in_sc[:], d["in_sc"]).then_inc(weights_in, 16)
                    sp.dma_start(out_sc[:], d["out_sc"]).then_inc(weights_in, 16)
                    sp.dma_start(bias1[:], d["b1"].rearrange("(o n) -> o n", o=1).to_broadcast([P, D]))\
                        .then_inc(weights_in, 16)
            for i in range(2):
                sp.wait_ge(wo_low, NW - 1 + i)
                raw_heads(0, i)
            for c in range(DC):
                if c:
                    sp.wait_ge(sign_ready, 2 * c)
                sp.dma_start(x1b[:], d["wb"][:, c, :]).then_inc(wb_in, 16)
            sp.wait_ge(sign_ready, 2 * DC)

            def body(tile, u):
                for i in range(2):
                    sp.wait_ge(oT_low, tile * PARTS + 2 * i + 2)
                    raw_heads(tile + 1, i)
                if not zero(tile):
                    sp.wait_ge(fin_ready, tile)
                    sp.dma_start(d["out"][bass.ds((tile - 1) * P, P), :], att[:]).then_inc(fin_out, 16)
                sp.dma_start(x1b[:], d["x1"][bass.ds(tile * P, P), :]).then_inc(x1_in, 16)

            body(0, 0)
            with sp.Fori(1, NT - 1) as tile:
                body(tile, 0)
            sp.wait_ge(fin_ready, NT - 1)
            sp.dma_start(d["out"][(NT - 2) * P:(NT - 1) * P, :], att[:]).then_inc(fin_out, 16)
            sp.dma_start(x1b[:], d["x1"][(NT - 1) * P:NT * P, :]).then_inc(x1_in, 16)
            sp.wait_ge(fin_ready, NT)
            sp.dma_start(d["out"][(NT - 1) * P:NT * P, :], att[:]).then_inc(fin_out, 16)
            sp.wait_ge(fin_out, 16 * NT)

        @block.gpsimd
        def _(pool):
            pool.wait_ge(weights_in, 16 * 4)

            def add(tile):
                pool.wait_ge(scaled, tile + 1)
                nc.gpsimd.tensor_tensor(att[:], att[:], bias1[:], ALU.add).then_inc(biased, 1)
                pool.wait_ge(biased, tile + 1)
                pool.wait_ge(x1_in, 16 * (tile + 1))
                nc.gpsimd.tensor_tensor(att[:], att[:], x1b[:], ALU.add).then_inc(fin_ready, 1)

            add(0)
            with pool.Fori(1, NT) as tile:
                add(tile)

        @block.tensor
        def _(pe):
            def product(tile, u, k):
                if k % 4 == 0:
                    pe.wait_ge(oT_low, tile * PARTS + k // 4 + 1)
                if k == 0 and not zero(tile, 2):
                    pe.wait_ge(att_ready, tile - 1)
                for h in (2 * k, 2 * k + 1):
                    mm = split3(pe, psW[u][:], (oThi[:, h, :], oTlo[:, h, :]), (wohi[:, h, :], wolo[:, h, :]),
                                h == 0, h == HQ - 1)
                if k % 4 == 3:
                    mm.then_inc(wo_mm, 1)

            def ffn(tile, k):
                if k == 1:
                    pe.wait_ge(att_ready, tile + 1)
                    if not zero(tile):
                        pe.wait_ge(osc_ready, tile)
                    for c in range(DC):
                        mm = pe.transpose(psF[:, c * P:(c + 1) * P], att[:, c * P:(c + 1) * P], t["ident"][:])
                    mm.then_inc(attT_mm, 1)
                if k == 3:
                    pe.wait_ge(attT_ready, tile + 1)
                    for c in range(DC):
                        mm = pe.matmul(psF[:, 0:NE], attT[:, c * P:(c + 1) * P], gate[:, c, :],
                                       start=(c == 0), stop=(c == DC - 1))
                    mm.then_inc(logit_mm, 1)
                if k == 6:
                    pe.wait_ge(route_ready, tile + 1)
                    pe.transpose(psF[0:NE, 0:P], route[:], t["ident"][:]).then_inc(routeT_mm, 1)
                if k == 8:
                    pe.wait_ge(routeT_ready, tile + 1)
                    for c in range(DC):
                        mm = pe.matmul(psF[:, c * P:(c + 1) * P], in_sc[:, c * P:(c + 1) * P], routeT[:],
                                       start=True, stop=True)
                    mm.then_inc(in_mm, 1)
                if k == 11:
                    pe.wait_ge(zlo_ready, tile + 1)
                    pe.matmul(psF[:], routeT[:], out_sc[:], start=True, stop=True).then_inc(out_mm, 1)
                    if not zero(tile):
                        pe.wait_ge(scaled, tile)
                    for c in range(DC):
                        pe.matmul(psZ[:], zhi[:, c * P:(c + 1) * P], wb[:, c, :], start=(c == 0), stop=False)
                        mm = pe.matmul(psZ[:], zlo[:, c * P:(c + 1) * P], wb[:, c, :], start=False, stop=(c == DC - 1))
                    mm.then_inc(ffn_mm, 1)

            pe.wait_ge(wo_low, NW)
            for k in range(16):
                product(0, 0, k)
            pe.wait_ge(weights_in, 16 * 4)
            pe.wait_ge(sign_ready, 2 * DC)

            def body(tile, u):
                for k in range(16):
                    product(tile, u, k)
                    ffn(tile - 1, k)

            body(1, 1)
            with pe.Fori(1, NT // 2) as pair:
                for u in range(2):
                    body(pair * 2 + u, u)
            for k in range(12):
                ffn(NT - 1, k)

        @block.scalar
        def _(act):
            for k in range(NW):
                act.wait_ge(raw_in[k % 2], 16 * (k // 2 + 1))
                nc.scalar.activation(wohi[:, k * WR:(k + 1) * WR, :].rearrange("p h n -> p (h n)"), raw[k % 2][:],
                                     ACT.Copy).then_inc(wo_high, 1)

            def high(tile, u, q):
                i = q // 2
                if q % 2 == 0:
                    act.wait_ge(raw_in[i], RAW0 + 16 * (tile + 1))
                if not zero(tile):
                    act.wait_ge(wo_mm, (tile - 1) * PARTS + q + 1)
                src = raw[i][:].rearrange("p (j h s) -> p j h s", j=BT, s=S)[:, :, (q % 2) * HP:(q % 2 + 1) * HP, :]
                for j in range(BT):
                    ins = nc.scalar.activation(oThi[:, q * HP:(q + 1) * HP, j * S:(j + 1) * S], src[:, j, :, :], ACT.Copy)
                ins.then_inc(oT_high, 1)

            def ffn(tile, u, k):
                if k == 0:
                    act.wait_ge(wo_mm, (tile + 1) * PARTS)
                    if not zero(tile):
                        act.wait_ge(fin_out, 16 * tile)
                    nc.scalar.activation(att[:], psW[u][:], ACT.Copy).then_inc(att_ready, 1)
                if k == 1:
                    act.wait_ge(attT_mm, tile + 1)
                    if not zero(tile):
                        act.wait_ge(zlo_ready, tile)
                    nc.scalar.activation(attT[:], psF[:], ACT.Copy).then_inc(attT_ready, 1)
                if k == 2:
                    act.wait_ge(rneg_ready, tile + 1)
                    nc.scalar.activation(rex[:], psF[:, 0:NE], ACT.Exp, bias=rneg[:, 0:1], accum_out=rsum[:, 0:1])\
                        .then_inc(rex_ready, 1)
                if k == 3:
                    act.wait_ge(routeT_mm, tile + 1)
                    nc.scalar.activation(routeT[:], psF[0:NE, 0:P], ACT.Copy).then_inc(routeT_ready, 1)
                if k == 4:
                    act.wait_ge(z_ready, tile + 1)
                    if not zero(tile):
                        act.wait_ge(ffn_mm, tile)
                    nc.scalar.activation(zhi[:], attT[:], ACT.Copy).then_inc(zhi_ready, 1)
                if k == 5:
                    act.wait_ge(out_mm, tile + 1)
                    nc.scalar.activation(att[:], psF[:], ACT.Copy).then_inc(osc_ready, 1)

            after = {0: 1, 1: 3, 2: 4, 3: 5}
            for q in range(PARTS):
                high(0, 0, q)
            for q in range(PARTS):
                high(1, 1, q)

            def body(tile, u):
                for k in range(6):
                    ffn(tile, u, k)
                    for q in range(PARTS):
                        if after[q] == k and not (isinstance(tile, int) and tile >= NT - 2):
                            high(tile + 2, u, q)

            body(0, 0)
            body(1, 1)
            with act.Fori(1, NT // 2 - 1) as pair:
                for u in range(2):
                    body(pair * 2 + u, u)
            body(NT - 2, 0)
            body(NT - 1, 1)

        @block.vector
        def _(dve):
            for k in range(NW):
                dve.wait_ge(wo_high, k + 1)
                part = slice(k * WR, (k + 1) * WR)
                nc.vector.tensor_tensor(wolo[:, part, :].rearrange("p h n -> p (h n)"), raw[k % 2][:],
                                        wohi[:, part, :].rearrange("p h n -> p (h n)").bitcast(F32), ALU.subtract)\
                    .then_inc(wo_low, 1)

            def low(tile, q):
                i = q // 2
                dve.wait_ge(oT_high, tile * PARTS + q + 1)
                src = raw[i][:].rearrange("p (j h s) -> p j h s", j=BT, s=S)[:, :, (q % 2) * HP:(q % 2 + 1) * HP, :]
                for j in range(BT):
                    at = (slice(None), slice(q * HP, (q + 1) * HP), slice(j * S, (j + 1) * S))
                    ins = nc.vector.tensor_tensor(oTlo[at], src[:, j, :, :], oThi[at].bitcast(F32), ALU.subtract)
                ins.then_inc(oT_low, 1)

            for q in range(PARTS):
                low(0, q)
            for c in range(DC):
                dve.wait_ge(wb_in, 16 * (c + 1))
                nc.vector.tensor_scalar(att[:], x1b[:], 0.0, None, ALU.is_lt).then_inc(sign_ready, 1)
                dve.wait_ge(sign_ready, 2 * c + 1)
                nc.vector.scalar_tensor_tensor(out=wb[:, c, :], in0=x1b[:], scalar=0.0, in1=att[:],
                                               op0=ALU.is_gt, op1=ALU.subtract).then_inc(sign_ready, 1)
                dve.wait_ge(sign_ready, 2 * c + 2)
            for q in range(PARTS):
                low(1, q)

            def ffn(tile, k):
                if k == 2:
                    dve.wait_ge(logit_mm, tile + 1)
                    nc.vector.tensor_reduce(rneg[:], psF[:, 0:NE], AX.X, ALU.max, negate=True).then_inc(rneg_ready, 1)
                    dve.wait_ge(rex_ready, tile + 1)
                    nc.vector.reciprocal(rrec[:], rsum[:]).then_inc(rrec_ready, 1)
                    dve.wait_ge(rrec_ready, tile + 1)
                    nc.vector.tensor_scalar(route[:], rex[:], rrec[:, 0:1], None, ALU.mult).then_inc(route_ready, 1)
                if k == 3:
                    dve.wait_ge(in_mm, tile + 1)
                    nc.vector.tensor_tensor(attT[:], psF[:], attT[:], ALU.mult).then_inc(z_ready, 1)
                if k == 4:
                    dve.wait_ge(zhi_ready, tile + 1)
                    nc.vector.tensor_tensor(zlo[:], attT[:], zhi[:].bitcast(F32), ALU.subtract).then_inc(zlo_ready, 1)
                if k == 5:
                    dve.wait_ge(ffn_mm, tile + 1)
                    dve.wait_ge(osc_ready, tile + 1)
                    nc.vector.tensor_tensor(att[:], psZ[:], att[:], ALU.mult).then_inc(scaled, 1)

            after = {0: 2, 1: 3, 2: 4, 3: 5}

            def body(tile, u):
                for k in range(2, 6):
                    ffn(tile, k)
                    for q in range(PARTS):
                        if after[q] == k and not (isinstance(tile, int) and tile >= NT - 2):
                            low(tile + 2, q)

            body(0, 0)
            body(1, 1)
            with dve.Fori(1, NT // 2 - 1) as pair:
                for u in range(2):
                    body(pair * 2 + u, u)
            body(NT - 2, 0)
            body(NT - 1, 1)


def adaln_ffn_program(nc, d):
    with ExitStack() as ctx:
        def sb(name, shape, dt=F32):
            return ctx.enter_context(nc.sbuf_tensor(name, shape, dt))

        t = {
            "ident": sb("ident", [P, P]),
            "cached": sb("cached", [P, B]),
            "key_no": sb("key_no", [P, L], mybir.dt.float16),
            "vrows": sb("vrows", [P, B, G4], I32),
        }
        with ExitStack() as early:
            def sbe(name, shape, dt=F32):
                return early.enter_context(nc.sbuf_tensor(name, shape, dt))

            t["xThi"] = sbe("xThi", [P, DC, B * S], F32R)
            t["xTlo"] = sbe("xTlo", [P, DC, B * S], F32R)
            for name in ("cosq", "sinq", "cosk", "sink"):
                t[name] = sbe(name, [P, NT, HD])
            with ExitStack() as first:
                def sbf(name, shape, dt=F32):
                    return first.enter_context(nc.sbuf_tensor(name, shape, dt))

                t["wsel"] = sbf("wsel", [P, NT, 2, P])
                t["bsel"] = sbf("bsel", [P, NT, 2])
                t["w2"] = sbf("w2", [P, 2 * S])
                t["bias0"] = sbf("bias0", [P, D])
                t["b2"] = sbf("b2", [P, S])
                t["tmask"] = sbf("tmask", [P, DC, B])
                constants(nc, t, d)
                layer0(nc, t, d)
            projections(nc, t, d)
        attention(nc, t, d)
        output_ffn(nc, t, d)


def kernel(**inputs):
    import concourse.bacc as bacc
    from concourse.bass_utils import run_bass_kernel_spmd

    def flat(name, shape):
        return np.asarray(inputs[name]).reshape(shape)

    def by_chunk(w):
        w = np.asarray(w)
        return w.T.reshape(-1, P, w.shape[0]).transpose(1, 0, 2)

    wqkv = np.concatenate([np.asarray(inputs[f"L1_cond_{n}"]) for n in ("Wq", "Wk", "Wv")])
    freq = (1.0 / np.float32(THETA) ** (np.arange(0, HD, 2, dtype=np.float32) / np.float32(HD))).astype(np.float32)
    arrays = {
        "x": flat("x", (B * S, D)),
        "ids": flat("itok_B_0_7", (B,)),
        "frames": flat("itok_B_2182_4065", (B,)),
        "table": flat("itok_Bx16_0_63", (B * NPP,)),
        "cached": flat("itok_B_207_1644", (B,)),
        "counts": flat("_lenS", (B,)),
        "freq": freq,
        "w_sess": flat("L0_cond_W_sess", (8, S, HID)),
        "b_sess": flat("L0_cond_b_sess", (8, HID)),
        "w2": flat("L0_cond_W2", (HID, S)),
        "b2": flat("L0_cond_b2", (S,)),
        "w0": by_chunk(inputs["L0_ffn_W"]),
        "b0": flat("L0_ffn_b", (D,)),
        "wq0": by_chunk(inputs["L0_ffn_Wq"]),
        "wk0": by_chunk(inputs["L0_ffn_Wk"]),
        "wa": by_chunk(flat("L0_ffn_A", (NE * RANK, D))),
        "bm": flat("L0_ffn_Bm", (NE, D, RANK)).transpose(0, 2, 1).reshape(NE * RANK, D),
        "wqkv": wqkv.reshape(-1, D, DC, P).transpose(0, 3, 2, 1),
        "qw": flat("L1_cond_q_norm_w", (HD,)),
        "kw": flat("L1_cond_k_norm_w", (HD,)),
        "kT": flat("L1_cond_k_cache", (PAGES, PSIZE, HK, HD)).transpose(0, 3, 2, 1).reshape(PAGES, HD, HK * PSIZE),
        "v": flat("L1_cond_v_cache", (PAGES * PSIZE, HK * HD)),
        "wo": flat("L1_cond_Wo", (D, HQ, HD)).transpose(2, 1, 0),
        "wb": by_chunk(inputs["L1_ffn_weight"]),
        "b1": flat("L1_ffn_bias", (D,)),
        "gate": by_chunk(inputs["L1_ffn_gate_w"]),
        "in_sc": flat("L1_ffn_in_channel_scale", (NE, D)),
        "out_sc": flat("L1_ffn_out_channel_scale", (NE, D)),
    }
    arrays = {name: np.ascontiguousarray(a) for name, a in arrays.items()}
    nc = bacc.Bacc("TRN2", target_bir_lowering=False, num_devices=1)
    d = {name: nc.dram_tensor(name + "_dram", a.shape, mybir.dt.from_np(a.dtype), kind="ExternalInput").ap()
         for name, a in arrays.items()}
    for name, shape in (("x1", (B * S, D)), ("qT", (B, HD, HQ * S)), ("kTn", (B, HD, HK * S)),
                        ("vn", (B * S, HK * HD)), ("oT", (B, HD, HQ * S))):
        d[name] = nc.dram_tensor(name + "_dram", shape, F32, kind="Internal").ap()
    d["out"] = nc.dram_tensor("out_dram", (B * S, D), F32, kind="ExternalOutput").ap()
    adaln_ffn_program(nc, d)
    result = run_bass_kernel_spmd(nc, [{name + "_dram": a for name, a in arrays.items()}], core_ids=[0])
    return result.results[0]["out_dram"].reshape(B, S, D)
```

```python
import math
from contextlib import ExitStack

import numpy as np

import concourse.bass as bass
from concourse import mybir

F32 = mybir.dt.float32
F32R = mybir.dt.float32r
I32 = mybir.dt.int32
ALU = mybir.AluOpType
ACT = mybir.ActivationFunctionType
AX = mybir.AxisListType

P = 128
B, S, D = 64, 32, 512
BT = P // S
NT = B // BT
DC = D // P
HID = 64
NE, DK, RANK = 8, 32, 16
HQ, HK, HD = 32, 8, 128
REP = HQ // HK
PAGES, PSIZE, NPP = 64, 32, 16
L = NPP * PSIZE
G4 = 4
THETA, EPS = 10000.0, 1e-6
SCALE = 1.0 / math.sqrt(HD)
MASKED = -1e30
WO_PIECE = 4
BIG = 3e38
PI2_A = 6.28125
PI2_B = 4058 / 2**21
PI2_C = 2 * math.pi - PI2_A - PI2_B
ROUND = 12582912.0


def started(turn):
    return not (isinstance(turn, int) and turn == 0)


def split3(pe, out, lhs, rhs, start, stop):
    pe.matmul(out, lhs[0], rhs[0], start=start, stop=False)
    pe.matmul(out, lhs[0], rhs[1], start=False, stop=False)
    return pe.matmul(out, lhs[1], rhs[0], start=False, stop=stop)


def tables(nc, t, d):
    with ExitStack() as ctx:
        def sb(name, shape, dt=F32):
            return ctx.enter_context(nc.sbuf_tensor(name, shape, dt))

        def sem(name):
            return ctx.enter_context(nc.semaphore(name))

        ids_i = sb("ids_i", [P, B], I32)
        counts_i = sb("counts_i", [P, B], I32)
        table_i = sb("table_i", [P, B * NPP], I32)
        frames_i = sb("frames_i", [P, B], I32)
        cached_i = sb("cached_i", [P, B], I32)
        chan_i = sb("chan_i", [P, 1], I32)
        time_i = sb("time_i", [P, DC], I32)
        key_i = sb("key_i", [P, L], I32)
        slots = sb("slots", [P, BT])
        chan_f = sb("chan_f", [P, 1])
        ids_f = sb("ids_f", [P, B])
        id_f = sb("id_f", [P, NT])
        count_f = sb("count_f", [P, NT])
        seen = sb("seen", [P, NT])
        frames_f = sb("frames_f", [P, B])
        time_f = sb("time_f", [P, DC])
        start_f = sb("start_f", [P, NT])
        pages_f = sb("pages_f", [P, B, G4])

        ids_in = sem("c_ids_in")
        loaded = sem("c_loaded")
        made = sem("c_made")
        zeroed = sem("c_zeroed")
        slots_made = sem("c_slots_made")
        step = sem("c_step")

        block = ctx.enter_context(nc.Block())
        n_loads = [0]

        @block.sync
        def _(sp):
            def everywhere(dst, src):
                return sp.dma_start(dst[:], src.rearrange("(o n) -> o n", o=1).to_broadcast([dst.shape[0], src.shape[0]]))

            everywhere(ids_i, d["ids"]).then_inc(ids_in, 16)
            for dst, src in ((counts_i, d["counts"]), (table_i, d["table"]), (frames_i, d["frames"]),
                             (cached_i, d["cached"])):
                n_loads[0] += 1
                everywhere(dst, src).then_inc(loaded, 16)
            sp.wait_ge(zeroed, 1)
            for i in range(2):
                sp.dma_start(t["bs"][:, i, :], d["b_sess"]).then_inc(t["small_in"], 16)
                sp.dma_start(t["w2"][i * HID:(i + 1) * HID, i * S:(i + 1) * S], d["w2"]).then_inc(t["small_in"], 16)
            for dst, src in ((t["b2"], d["b2"]), (t["freq"], d["freq"]), (t["qw"], d["qw"]), (t["kw"], d["kw"]),
                             (t["bias0"], d["b0"])):
                everywhere(dst, src).then_inc(t["small_in"], 16)

        @block.vector
        def _(dve):
            done = [0]

            def then(ins):
                done[0] += 1
                ins.then_inc(step, 1)
                dve.wait_ge(step, done[0])

            def of_tile(dst, src):
                for j in range(BT):
                    rows = slice(j * S, (j + 1) * S)
                    ins = nc.vector.tensor_copy(dst[rows, :], src[rows, :].rearrange("p (t j) -> p t j", j=BT)[:, :, j])
                return ins

            dve.wait_ge(made, 5)
            dve.wait_ge(ids_in, 16)
            then(nc.vector.tensor_copy(ids_f[:], ids_i[:]))
            then(nc.vector.tensor_copy(chan_f[:], chan_i[:]))
            then(nc.vector.tensor_scalar(t["onehot"][:], ids_f[0:8, :], chan_f[0:8, 0:1], None, ALU.is_equal))
            then(nc.vector.tensor_scalar(chan_i[:], chan_i[:], S - 1, None, ALU.bitwise_and))
            then(nc.vector.tensor_copy(chan_f[:], chan_i[:]))
            then(of_tile(id_f, ids_f))
            then(nc.vector.tensor_scalar(id_f[:], id_f[:], float(S), chan_f[:, 0:1], ALU.mult, ALU.add))
            then(nc.vector.tensor_copy(t["wrows"][:], id_f[:]))
            dve.wait_ge(loaded, 16 * n_loads[0])
            then(of_tile(count_f, counts_i))
            then(nc.vector.tensor_scalar(seen[:], count_f[:], chan_f[:, 0:1], None, ALU.is_gt))
            dve.wait_ge(slots_made, BT)
            then(nc.vector.tensor_tensor(t["seen4"][:], slots[:].unsqueeze(1).to_broadcast([P, NT, BT]),
                                         seen[:].unsqueeze(2).to_broadcast([P, NT, BT]), ALU.mult))
            then(nc.vector.tensor_copy(time_f[:], time_i[:]))
            then(nc.vector.tensor_copy(frames_f[:], frames_i[:]))
            for c in range(DC):
                then(nc.vector.tensor_scalar(t["tmask"][:, c, :], frames_f[:], time_f[:, c:c + 1], None, ALU.is_gt))
            then(of_tile(start_f, cached_i))
            then(nc.vector.tensor_scalar(t["pos"][:], start_f[:], chan_f[:, 0:1], None, ALU.add))
            then(nc.vector.tensor_copy(t["cached"][:], cached_i[:]))
            then(nc.vector.tensor_copy(t["key_no"][:], key_i[:]))
            for j in range(G4):
                rows = slice(j * S, (j + 1) * S)
                then(nc.vector.tensor_copy(pages_f[rows, :, :],
                                           table_i[rows, :].rearrange("p (b c j) -> p b c j", j=G4, b=B)[:, :, :, j]))
            then(nc.vector.tensor_scalar(pages_f[:], pages_f[:], float(PSIZE), chan_f[:, 0:1], ALU.mult, ALU.add))
            then(nc.vector.tensor_copy(t["vrows"][:], pages_f[:]))

        @block.gpsimd
        def _(pool):
            nc.gpsimd.memset(t["w2"][:], 0.0).then_inc(zeroed, 1)
            nc.gpsimd.iota(chan_i[:], pattern=[[0, 1]], base=0, channel_multiplier=1).then_inc(made, 1)
            nc.gpsimd.iota(time_i[:], pattern=[[P, DC]], base=0, channel_multiplier=1).then_inc(made, 1)
            nc.gpsimd.iota(key_i[:], pattern=[[1, L]], base=0, channel_multiplier=0).then_inc(made, 1)
            nc.gpsimd.memset(t["ident"][:], 0.0).then_inc(made, 1)
            nc.gpsimd.memset(slots[:], 0.0).then_inc(made, 1)
            pool.wait_ge(made, 5)
            for j in range(BT):
                nc.gpsimd.memset(slots[j * S:(j + 1) * S, j:j + 1], 1.0).then_inc(slots_made, 1)
            pool.wait_ge(slots_made, BT)
            nc.gpsimd.affine_select(out=t["ident"][:], in_=t["ident"][:], compare_op=ALU.not_equal, fill=1.0,
                                    base=0, pattern=[[-1, P]], channel_multiplier=1).then_inc(made, 1)


def pairs(eng, body):
    for u in range(2):
        body(u, u, 0)
    with eng.Fori(1, NT // 2 - 1) as pair:
        for u in range(2):
            body(pair * 2 + u, u, pair)
    for u in range(2):
        body(NT - 2 + u, u, NT // 2 - 1)


def below(tile, n):
    return isinstance(tile, int) and tile < n


def among_last(tile, n):
    return isinstance(tile, int) and tile >= NT - n


def sessions(nc, t, d):
    with ExitStack() as ctx:
        def sb(name, shape, dt=F32):
            return ctx.enter_context(nc.sbuf_tensor(name, shape, dt))

        def ps(name, shape):
            return ctx.enter_context(nc.psum_tensor(name, shape, F32))

        def sem(name):
            return ctx.enter_context(nc.semaphore(name))

        xt = [sb(f"s_xt{i}", [P, D]) for i in range(2)]
        wcur = [sb(f"wcur{i}", [P, BT, HID]) for i in range(2)]
        hid = [[sb(f"hid{i}_{k}", [P, D]) for k in range(2)] for i in range(2)]
        bsel = sb("bsel", [P, NT * 2])
        angle, turn = t["cosq"][:, :, 0:HD // 2], t["cosq"][:, :, HD // 2:HD]
        turn2, part2 = t["cosk"][:, :, 0:HD // 2], t["cosk"][:, :, HD // 2:HD]
        ypre = sb("ypre", [P, DC, BT, S])

        psH = [[ps(f"psH{i}_{k}", [P, D]) for k in range(2)] for i in range(2)]
        psY = [ps(f"psY{i}", [P, DC, BT, S]) for i in range(2)]
        psB = ps("psB", [P, B])

        x_in = [sem(f"s_x_in{i}") for i in range(2)]
        session_in = [sem(f"s_session_in{i}") for i in range(2)]
        bias_mm = sem("s_bias_mm")
        bias_ready = sem("s_bias_ready")
        wcur_ready = sem("s_wcur_ready")
        hid_mm = sem("s_hid_mm")
        hid_ready = sem("s_hid_ready")
        y_mm = sem("s_y_mm")
        ypre_ready = sem("s_ypre_ready")
        yT_ready = sem("s_yT_ready")
        angle_ready = sem("s_angle_ready")
        sine_step = sem("s_sine_step")
        cosine_step = sem("s_cosine_step")

        block = ctx.enter_context(nc.Block())

        def reduced_angle(eng, ops, step, quarter, out, turn, part):
            done = [0]

            def then(ins):
                done[0] += 1
                ins.then_inc(step, 1)
                eng.wait_ge(step, done[0])

            then(ops.tensor_scalar(turn, angle, 1 / (2 * math.pi), quarter, ALU.mult, ALU.add))
            then(ops.tensor_scalar(turn, turn, ROUND, -ROUND, ALU.add, ALU.add))
            for n, pi2 in enumerate((PI2_A, PI2_B, PI2_C)):
                then(ops.tensor_scalar(part, turn, -pi2, None, ALU.mult))
                then(ops.tensor_tensor(out[:], part, angle if n == 0 else out[:], ALU.add))
            then(ops.tensor_scalar(out[:], out[:], quarter * 2 * math.pi, 3.1415925, ALU.add, ALU.min))
            then(ops.tensor_scalar(out[:], out[:], -3.1415925, None, ALU.max))

        @block.sync
        def _(sp):
            def load(tile, u):
                if not below(tile, 2):
                    sp.wait_ge(hid_mm, tile - 1)
                sp.dma_start(xt[u][:], d["x"][bass.ds(tile * P, P), :]).then_inc(x_in[u], 16)

            for u in range(2):
                load(u, u)
            sp.dma_start(t["w0"][:], d["w0"]).then_inc(t["weights_in"], 16)
            sp.dma_start(t["wqk"][:, :, 0, :], d["wq0"]).then_inc(t["weights_in"], 16)
            sp.dma_start(t["wqk"][:, :, 1, :], d["wk0"]).then_inc(t["weights_in"], 16)
            sp.dma_start(t["wa"][:], d["wa"]).then_inc(t["weights_in"], 16)
            sp.dma_start(t["bm"][:], d["bm"]).then_inc(t["weights_in"], 16)
            with sp.Fori(1, NT // 2) as pair:
                for u in range(2):
                    load(pair * 2 + u, u)

        @block.gpsimd
        def _(pool):
            for tile in range(NT):
                if tile >= 2:
                    pool.wait_ge(session_in[tile % 2], 16 * (tile // 2))
                nc.gpsimd.indirect_dma_start(t["wsel"][:, tile, :], None, d["w_sess"],
                                             bass.IndirectOffsetOnAxis(t["wrows"][:, tile:tile + 1], 0))\
                    .then_inc(session_in[tile % 2], 16)

            pool.wait_ge(angle_ready, 1)
            reduced_angle(pool, nc.gpsimd, cosine_step, 0.25, t["cos"], turn2, part2)

        @block.tensor
        def _(pe):
            def hidden(tile, u, turn):
                pe.wait_ge(x_in[u], 16 * (turn + 1))
                pe.wait_ge(wcur_ready, tile + 1)
                if not below(tile, 2):
                    pe.wait_ge(hid_ready, tile - 1)
                for k in range(2):
                    mm = pe.matmul(psH[u][k][:], wcur[u][:, 2 * k:2 * k + 2, :].rearrange("p j h -> p (j h)"), xt[u][:],
                                   start=True, stop=True)
                mm.then_inc(hid_mm, 1)

            def body(tile, u, turn):
                if not among_last(tile, 1):
                    hidden(tile + 1, 1 - u, turn + u)
                pe.wait_ge(hid_ready, tile + 1)
                if not below(tile, 2):
                    pe.wait_ge(ypre_ready, tile - 1)
                for c in range(DC):
                    for k in range(2):
                        mm = pe.matmul(psY[u][:, c, 2 * k:2 * k + 2, :], hid[u][k][:, c * P:(c + 1) * P], t["w2"][:],
                                       start=True, stop=True)
                mm.then_inc(y_mm, 1)

            pe.wait_ge(t["small_in"], 16 * t["smalls"])
            pe.matmul(psB[:], t["bs"][:].rearrange("s i h -> s (i h)"), t["onehot"][:], start=True, stop=True)\
                .then_inc(bias_mm, 1)
            hidden(0, 0, 0)
            pairs(pe, body)

        @block.scalar
        def _(act):
            def body(tile, u, turn):
                act.wait_ge(hid_mm, tile + 1)
                if not below(tile, 2):
                    act.wait_ge(y_mm, tile - 1)
                for k in range(2):
                    ins = nc.scalar.activation(hid[u][k][:], psH[u][k][:], ACT.Gelu,
                                               bias=bsel[:, bass.ds(tile * 2 + k, 1)])
                ins.then_inc(hid_ready, 1)

            act.wait_ge(bias_ready, 2)
            pairs(act, body)

        @block.vector
        def _(dve):
            def weights(tile, u, turn):
                if not below(tile, 2):
                    dve.wait_ge(hid_mm, tile - 1)
                dve.wait_ge(session_in[u], 16 * (turn + 1))
                nc.vector.tensor_tensor(wcur[u][:],
                                        t["wsel"][:, bass.ds(tile, 1), :].to_broadcast([P, BT, HID]),
                                        t["seen4"][:, bass.ds(tile, 1), :].rearrange("p a j -> p (a j)").unsqueeze(2)
                                        .to_broadcast([P, BT, HID]), ALU.mult).then_inc(wcur_ready, 1)

            def body(tile, u, turn):
                if not among_last(tile, 2):
                    weights(tile + 2, u, turn + 1)
                dve.wait_ge(y_mm, tile + 1)
                nc.vector.tensor_tensor(ypre[:], psY[u][:],
                                        t["b2"][:].unsqueeze(1).unsqueeze(1).to_broadcast([P, DC, BT, S]),
                                        ALU.add).then_inc(ypre_ready, 1)
                dve.wait_ge(ypre_ready, tile + 1)
                nc.vector.tensor_tensor(t["yT"][:, :, bass.ds(tile * P, P)].rearrange("p c (b s) -> p c b s", s=S), ypre[:],
                                        t["tmask"][:, :, bass.ds(tile * BT, BT)].unsqueeze(3)
                                        .to_broadcast([P, DC, BT, S]), ALU.mult).then_inc(yT_ready, 1)
                dve.wait_ge(yT_ready, tile + 1)

            dve.wait_ge(bias_mm, 1)
            for i in range(2):
                half = slice(i * HID, (i + 1) * HID)
                nc.vector.tensor_copy(bsel[half, :], psB[half, :].rearrange("p (n i) -> p n i", i=2)[:, :, i])\
                    .then_inc(bias_ready, 1)
            for u in range(2):
                weights(u, u, 0)
            nc.vector.tensor_tensor(angle, t["pos"][:].unsqueeze(2).to_broadcast([P, NT, HD // 2]),
                                    t["freq"][:].unsqueeze(1).to_broadcast([P, NT, HD // 2]), ALU.mult)\
                .then_inc(angle_ready, 1)
            dve.wait_ge(angle_ready, 1)
            reduced_angle(dve, nc.vector, sine_step, 0.0, t["sin"], turn, t["part"][:])
            pairs(dve, body)


def layer0(nc, t, d):
    with ExitStack() as ctx:
        def sb(name, shape, dt=F32):
            return ctx.enter_context(nc.sbuf_tensor(name, shape, dt))

        def ps(name, shape):
            return ctx.enter_context(nc.psum_tensor(name, shape, F32))

        def sem(name):
            return ctx.enter_context(nc.semaphore(name))

        xt = [sb(f"xt{i}", [P, D]) for i in range(2)]
        x1 = [sb(f"x1_{i}", [P, D]) for i in range(2)]
        yt = [sb(f"yt{i}", [P, DC, P]) for i in range(2)]
        kk = sb("kk", [P, NE * DK])
        prod = sb("prod", [P, NE * DK])
        sc = sb("sc", [P, NE])
        negm = sb("negm", [P, 1])
        ex = sb("ex", [P, NE])
        tot = sb("tot", [P, 1])
        rtot = sb("rtot", [P, 1])
        wn = sb("wn", [P, NE])
        wh = sb("wh", [P, NE, RANK])
        whT = sb("whT", [P, P])

        psR = [ps(f"psR{i}", [P, D]) for i in range(2)]
        psQK = ps("psQK", [P, 2, NE * DK])
        psA = ps("psA", [P, NE, RANK])
        psT = ps("psT", [P, P])
        psX = ps("psX", [P, DC, P])

        x_in = [sem(f"l0_x_in{i}") for i in range(2)]
        x1_out = [sem(f"l0_x1_out{i}") for i in range(2)]
        yt_ready = sem("l0_yt_ready")
        qk_mm = sem("l0_qk_mm")
        kk_ready = sem("l0_kk_ready")
        prod_ready = sem("l0_prod_ready")
        sc_ready = sem("l0_sc_ready")
        negm_ready = sem("l0_negm_ready")
        ex_ready = sem("l0_ex_ready")
        rtot_ready = sem("l0_rtot_ready")
        wn_ready = sem("l0_wn_ready")
        wh_ready = sem("l0_wh_ready")
        whT_mm = sem("l0_whT_mm")
        whT_ready = sem("l0_whT_ready")
        sum_mm = sem("l0_sum_mm")
        xb_ready = sem("l0_xb_ready")
        x1_ready = sem("l0_x1_ready")
        xT_mm = sem("l0_xT_mm")
        hi_ready = sem("l0_hi_ready")
        lo_ready = sem("l0_lo_ready")
        sines = sem("l0_sines")
        table_step = sem("l0_table_step")

        block = ctx.enter_context(nc.Block())

        @block.sync
        def _(sp):
            def load(tile, u):
                if not below(tile, 2):
                    sp.wait_ge(xb_ready, tile - 1)
                sp.dma_start(xt[u][:], d["x"][bass.ds(tile * P, P), :]).then_inc(x_in[u], 16)

            def body(tile, u, turn):
                if not among_last(tile, 2):
                    load(tile + 2, u)
                sp.wait_ge(x1_ready, tile + 1)
                sp.dma_start(d["x1"][bass.ds(tile * P, P), :], x1[u][:]).then_inc(x1_out[u], 16)

            for u in range(2):
                load(u, u)
            for w in range(2):
                sp.dma_start(t["wraw"][w][:], d["wqkv"][w, :, :, :]).then_inc(t["wraw_in"][w], 16)
            pairs(sp, body)
            for u in range(2):
                sp.wait_ge(x1_out[u], 16 * (NT // 2))

        @block.gpsimd
        def _(pool):
            done = [0]

            def then(ins):
                done[0] += 1
                ins.then_inc(table_step, 1)
                pool.wait_ge(table_step, done[0])

            pool.wait_ge(sines, 2)
            half = HD // 2
            for w, ca, sa in ((t["qw"], t["cosq"], t["sinq"]), (t["kw"], t["cosk"], t["sink"])):
                w1 = w[:, 0:half].unsqueeze(1).to_broadcast([P, NT, half])
                w2 = w[:, half:HD].unsqueeze(1).to_broadcast([P, NT, half])
                then(nc.gpsimd.tensor_tensor(ca[:, :, 0:half], t["cos"][:], w1, ALU.mult))
                then(nc.gpsimd.tensor_tensor(ca[:, :, half:HD], t["cos"][:], w2, ALU.mult))
                then(nc.gpsimd.tensor_tensor(sa[:, :, half:HD], t["sin"][:], w1, ALU.mult))
                then(nc.gpsimd.tensor_tensor(t["part"][:], t["sin"][:], w2, ALU.mult))
                then(nc.gpsimd.tensor_scalar(sa[:, :, 0:half], t["part"][:], -1.0, None, ALU.mult))

        @block.tensor
        def _(pe):
            def x1_transposes(tile, u):
                pe.wait_ge(x1_ready, tile + 1)
                if not below(tile, 1):
                    pe.wait_ge(lo_ready, tile)
                for c in range(DC):
                    mm = pe.transpose(psX[:, c, :], x1[u][:, c * P:(c + 1) * P], t["ident"][:])
                mm.then_inc(xT_mm, 1)

            def body(tile, u, turn):
                pe.wait_ge(yt_ready, tile + 1)
                for c in range(DC):
                    pe.matmul(psQK[:].rearrange("p a n -> p (a n)"), yt[u][:, c, :],
                              t["wqk"][:, c, :, :].rearrange("p a n -> p (a n)"), start=(c == 0), stop=(c == DC - 1))
                for c in range(DC):
                    mm = pe.matmul(psA[:].rearrange("p e r -> p (e r)"), yt[u][:, c, :], t["wa"][:, c, :],
                                   start=(c == 0), stop=(c == DC - 1))
                mm.then_inc(qk_mm, 1)
                if not below(tile, 2):
                    pe.wait_ge(x1_ready, tile - 1)
                for c in range(DC):
                    pe.matmul(psR[u][:], yt[u][:, c, :], t["w0"][:, c, :], start=(c == 0), stop=False)
                pe.wait_ge(wh_ready, tile + 1)
                pe.transpose(psT[:], wh[:].rearrange("p e r -> p (e r)"), t["ident"][:]).then_inc(whT_mm, 1)
                if not below(tile, 1):
                    x1_transposes(tile - 1, 1 - u)
                pe.wait_ge(whT_ready, tile + 1)
                pe.matmul(psR[u][:], whT[:], t["bm"][:], start=False, stop=True).then_inc(sum_mm, 1)

            pe.wait_ge(t["weights_in"], 16 * 5)
            pairs(pe, body)
            x1_transposes(NT - 1, 1)

        @block.scalar
        def _(act):
            def tile_sources(tile, u):
                if not below(tile, 2):
                    act.wait_ge(sum_mm, tile - 1)
                nc.scalar.activation(yt[u][:], t["yT"][:, :, bass.ds(tile * P, P)], ACT.Copy).then_inc(yt_ready, 1)

            def high(tile):
                act.wait_ge(xT_mm, tile + 1)
                nc.scalar.activation(t["xThi"][:, :, bass.ds(tile * P, P)], psX[:], ACT.Copy).then_inc(hi_ready, 1)

            def body(tile, u, turn):
                act.wait_ge(qk_mm, tile + 1)
                nc.scalar.activation(kk[:], psQK[:, 1, :], ACT.Copy, scale=1.0 / math.sqrt(DK)).then_inc(kk_ready, 1)
                if not among_last(tile, 1):
                    tile_sources(tile + 1, 1 - u)
                act.wait_ge(negm_ready, tile + 1)
                nc.scalar.activation(ex[:], sc[:], ACT.Exp, bias=negm[:, 0:1], accum_out=tot[:, 0:1]).then_inc(ex_ready, 1)
                act.wait_ge(whT_mm, tile + 1)
                nc.scalar.activation(whT[:], psT[:], ACT.Copy).then_inc(whT_ready, 1)
                if not below(tile, 1):
                    high(tile - 1)

            tile_sources(0, 0)
            for angle in (t["sin"], t["cos"]):
                nc.scalar.activation(angle[:], angle[:], ACT.Sin).then_inc(sines, 1)
            pairs(act, body)
            high(NT - 1)

        @block.vector
        def _(dve):
            def low(tile):
                dve.wait_ge(hi_ready, tile + 1)
                nc.vector.tensor_tensor(t["xTlo"][:, :, bass.ds(tile * P, P)], psX[:],
                                        t["xThi"][:, :, bass.ds(tile * P, P)].bitcast(F32),
                                        ALU.subtract).then_inc(lo_ready, 1)

            def residual(tile, u, turn):
                dve.wait_ge(x_in[u], 16 * (turn + 1))
                if not below(tile, 2):
                    dve.wait_ge(x1_out[u], 16 * turn)
                    dve.wait_ge(xT_mm, tile - 1)
                nc.vector.tensor_tensor(x1[u][:], xt[u][:], t["bias0"][:], ALU.add).then_inc(xb_ready, 1)

            def body(tile, u, turn):
                dve.wait_ge(kk_ready, tile + 1)
                nc.vector.tensor_tensor(prod[:], psQK[:, 0, :], kk[:], ALU.mult).then_inc(prod_ready, 1)
                dve.wait_ge(prod_ready, tile + 1)
                nc.vector.reduce_sum(sc[:], prod[:].rearrange("p (e k) -> p e k", k=DK), AX.X).then_inc(sc_ready, 1)
                dve.wait_ge(sc_ready, tile + 1)
                nc.vector.tensor_reduce(negm[:], sc[:], AX.X, ALU.max, negate=True).then_inc(negm_ready, 1)
                dve.wait_ge(ex_ready, tile + 1)
                nc.vector.reciprocal(rtot[:], tot[:]).then_inc(rtot_ready, 1)
                dve.wait_ge(rtot_ready, tile + 1)
                nc.vector.tensor_scalar(wn[:], ex[:], rtot[:, 0:1], None, ALU.mult).then_inc(wn_ready, 1)
                dve.wait_ge(wn_ready, tile + 1)
                nc.vector.tensor_tensor(wh[:], psA[:], wn[:].unsqueeze(2).to_broadcast([P, NE, RANK]),
                                        ALU.mult).then_inc(wh_ready, 1)
                residual(tile, u, turn)
                if not below(tile, 1):
                    low(tile - 1)
                dve.wait_ge(xb_ready, tile + 1)
                dve.wait_ge(sum_mm, tile + 1)
                nc.vector.tensor_tensor(x1[u][:], psR[u][:], x1[u][:], ALU.add).then_inc(x1_ready, 1)

            pairs(dve, body)
            low(NT - 1)


def projections(nc, t, d):
    NQ, NKC = HQ * HD // D, HK * HD // D
    NG = NQ + 2 * NKC
    U = 4
    with ExitStack() as ctx:
        def sb(name, shape, dt=F32):
            return ctx.enter_context(nc.sbuf_tensor(name, shape, dt))

        def ps(name, shape):
            return ctx.enter_context(nc.psum_tensor(name, shape, F32))

        def sem(name):
            return ctx.enter_context(nc.semaphore(name))

        wraw = t["wraw"]
        whi = [sb(f"whi{i}", [P, DC, D], F32R) for i in range(2)]
        wlo = [sb(f"wlo{i}", [P, DC, D], F32R) for i in range(2)]
        squares = sb("squares", [P, G4, HD])
        eps = sb("eps", [P, 1])
        ssq = sb("ssq", [P, U, G4])
        std = sb("std", [P, U, G4])
        rstd = sb("rstd", [P, U, G4])
        straight = [sb(f"straight{i}", [P, G4, HD]) for i in range(2)]
        crossed = [sb(f"crossed{i}", [P, G4, HD]) for i in range(2)]
        turned = [sb(f"turned{i}", [P, G4, HD]) for i in range(U)]
        stage = [sb(f"stage{i}", [P, BT, G4, S]) for i in range(2)]
        psP = [ps(f"psP{i}", [P, G4, HD]) for i in range(U)]
        psTr = [ps(f"psTr{i}", [P, G4, BT, S]) for i in range(2)]

        w_in = t["wraw_in"]
        whi_ready = sem("p_whi_ready")
        wlo_ready = sem("p_wlo_ready")
        eps_ready = sem("p_eps_ready")
        proj_mm = sem("p_proj_mm")
        ssq_ready = sem("p_ssq_ready")
        std_ready = sem("p_std_ready")
        rstd_ready = sem("p_rstd_ready")
        parts_ready = sem("p_parts_ready")
        sum_ready = sem("p_sum_ready")
        turned_ready = sem("p_turned_ready")
        heads_mm = sem("p_heads_mm")
        stage_ready = sem("p_stage_ready")
        stored = [sem(f"p_stored{i}") for i in range(2)]

        block = ctx.enter_context(nc.Block())
        NN = (NQ + NKC) * NT

        def is_first(n, count):
            return isinstance(n, int) and n < count

        @block.sync
        def _(sp):
            def load(g, w):
                sp.dma_start(wraw[w][:], d["wqkv"][bass.ds(g, 1), :, :, :].rearrange("a p c n -> (a p) c n"))\
                    .then_inc(w_in[w], 16)

            def chunk(g, w, store):
                if not (isinstance(g, int) and g >= NG - 2):
                    sp.wait_ge(wlo_ready, g * DC + DC)
                    load(g + 2, w)
                with sp.Fori(0, NT // 2) as pair:
                    for u in range(2):
                        sp.wait_ge(stage_ready, g * NT + pair * 2 + u + 1)
                        store(g, pair * 2 + u, u)

            def queries(g, tile, u):
                dst = d["qT"].rearrange("(t j) p (g n) -> t g p j n", j=BT, g=NQ)
                sp.dma_start(dst[bass.ds(tile, 1), bass.ds(g, 1), :, :, :].rearrange("a b p j n -> (a b p) j n"),
                             stage[u][:].rearrange("p j h s -> p j (h s)")).then_inc(stored[u], 16)

            def keys(g, tile, u):
                dst = d["kTn"].rearrange("(t j) p (g n) -> t g p j n", j=BT, g=NKC)
                sp.dma_start(dst[bass.ds(tile, 1), bass.ds(g - NQ, 1), :, :, :].rearrange("a b p j n -> (a b p) j n"),
                             stage[u][:].rearrange("p j h s -> p j (h s)")).then_inc(stored[u], 16)

            def values(g, tile, u):
                sp.dma_start(d["vn"][bass.ds(tile * P, P), (g - NQ - NKC) * D:(g - NQ - NKC + 1) * D],
                             stage[u][:].rearrange("p j h s -> p (j h s)")).then_inc(stored[u], 16)

            with sp.Fori(0, NQ // 2) as pair:
                for w in range(2):
                    chunk(pair * 2 + w, w, queries)
            for w in range(2):
                chunk(NQ + w, w, keys)
            pages = [sp.alloc_register(f"page0_{k}") for k in range(NPP)]
            sp.load(pages, d["table"].rearrange("(o n) -> o n", o=1)[:, 0:NPP])
            for k in range(NPP):
                page = sp.snap(pages[k], min_val=0, max_val=PAGES - 1)
                sp.dma_start(t["kst0"][:, k, :, :].rearrange("p h n -> p (h n)"),
                             d["kT"][bass.ds(page, 1), :, :].rearrange("a p n -> (a p) n")).then_inc(t["k_in0"], 16)
            for w in range(2):
                chunk(NQ + NKC + w, w, values)
            for u in range(2):
                sp.wait_ge(stored[u], 16 * NG * NT // 2)

        @block.gpsimd
        def _(pool):
            nc.gpsimd.memset(eps[:], EPS).then_inc(eps_ready, 1)

            def body(turn, u):
                n = turn * U + u
                pool.wait_ge(parts_ready, n + 1)
                nc.gpsimd.tensor_tensor(straight[u % 2][:], straight[u % 2][:], crossed[u % 2][:], ALU.add)\
                    .then_inc(sum_ready, 1)
                if started(turn):
                    pool.wait_ge(heads_mm, n - 3)
                pool.wait_ge(sum_ready, n + 1)
                nc.gpsimd.tensor_tensor(turned[u][:], straight[u % 2][:],
                                        rstd[:, u, :].unsqueeze(2).to_broadcast([P, G4, HD]), ALU.mult)\
                    .then_inc(turned_ready, 1)

            for u in range(U):
                body(0, u)
            with pool.Fori(1, NN // U) as turn:
                for u in range(U):
                    body(turn, u)
            for c in range(L // P):
                nc.gpsimd.indirect_dma_start(t["vst0"][:, c, :], None, d["v"],
                                             bass.IndirectOffsetOnAxis(t["vrows"][:, 0, c:c + 1], 0))\
                    .then_inc(t["v_in0"], 16)

        @block.tensor
        def _(pe):
            def transposes(m, i):
                pe.wait_ge(turned_ready, m + 1)
                if not is_first(m, 2):
                    pe.wait_ge(stage_ready, m - 1)
                for h in range(G4):
                    mm = pe.transpose(psTr[i % 2][:, h, :, :].rearrange("p j s -> p (j s)"),
                                      turned[i % U][:, h, :], t["ident"][:])
                mm.then_inc(heads_mm, 1)

            def chunk(g, w, heads):
                if not is_first(g, 1):
                    pe.wait_ge(wlo_ready, g * DC + DC)
                for tile in range(NT):
                    n = g * NT + tile
                    if heads and not is_first(n, U):
                        pe.wait_ge(parts_ready, n - 3)
                    if not heads:
                        pe.wait_ge(stage_ready, n - 3)
                    cols = slice(tile * P, (tile + 1) * P)
                    for c in range(DC):
                        if is_first(n, 1):
                            pe.wait_ge(wlo_ready, c + 1)
                        mm = split3(pe, psP[tile % U][:].rearrange("p h n -> p (h n)"),
                                    (t["xThi"][:, c, cols], t["xTlo"][:, c, cols]),
                                    (whi[w][:, c, :], wlo[w][:, c, :]), c == 0, c == DC - 1)
                    mm.then_inc(proj_mm, 1)
                    if heads and not is_first(n, 2):
                        transposes(n - 2, tile + 2)

            for w in range(2):
                chunk(w, w, True)
            with pe.Fori(1, (NQ + NKC) // 2) as pair:
                for w in range(2):
                    chunk(pair * 2 + w, w, True)
            for i in range(2):
                transposes(NN - 2 + i, U - 2 + i)
            for w in range(2):
                chunk(NQ + NKC + w, w, False)

        @block.scalar
        def _(act):
            def weights(g, w, turn):
                act.wait_ge(w_in[w], 16 * (turn + 1))
                if started(turn):
                    act.wait_ge(proj_mm, (g - 1) * NT)
                for c in range(DC):
                    nc.scalar.activation(whi[w][:, c, :], wraw[w][:, c, :], ACT.Copy).then_inc(whi_ready, 1)

            def norms(turn, u):
                n = turn * U + u
                act.wait_ge(proj_mm, n + 1)
                for h in range(G4):
                    ins = nc.scalar.activation(squares[:, h, :], psP[u][:, h, :], ACT.Square,
                                               accum_out=ssq[:, u, h:h + 1])
                ins.then_inc(ssq_ready, 1)
                act.wait_ge(ssq_ready, n + 1)
                nc.scalar.activation(std[:, u, :], ssq[:, u, :], ACT.Sqrt, bias=eps[:, 0:1], scale=1.0 / HD)\
                    .then_inc(std_ready, 1)

            def copy_out(turn, u):
                m = turn * U + u - 2
                act.wait_ge(heads_mm, m + 1)
                if not is_first(m, 2):
                    act.wait_ge(stored[u % 2], 16 * (2 * turn + (u - 2) // 2))
                nc.scalar.activation(stage[u % 2][:].rearrange("p j h s -> p h j s"), psTr[u % 2][:], ACT.Copy)\
                    .then_inc(stage_ready, 1)

            def chunk(g, w, turn0, peel):
                weights(g + 1, 1 - w, turn0 + w)
                if peel:
                    for u in range(U):
                        norms(0, u)
                        if u >= 2:
                            copy_out(0, u)
                with act.Fori(1 if peel else 0, NT // U) as k:
                    for u in range(U):
                        norms(g * (NT // U) + k, u)
                        copy_out(g * (NT // U) + k, u)

            act.wait_ge(eps_ready, 1)
            weights(0, 0, 0)
            chunk(0, 0, 0, True)
            chunk(1, 1, 0, False)
            with act.Fori(1, (NQ + NKC) // 2) as pair:
                for w in range(2):
                    chunk(pair * 2 + w, w, pair, False)
            for u in range(2):
                copy_out(NN // U, u)
            weights(NG - 1, 1, NG // 2 - 1)
            with act.Fori(NN // U, NG * NT // U) as turn:
                for u in range(U):
                    n = turn * U + u
                    act.wait_ge(proj_mm, n + 1)
                    act.wait_ge(stored[u % 2], 16 * (2 * turn + u // 2))
                    nc.scalar.activation(stage[u % 2][:].rearrange("p j h s -> p (j h s)"),
                                         psP[u][:].rearrange("p h n -> p (h n)"), ACT.Copy)\
                        .then_inc(stage_ready, 1)

        @block.vector
        def _(dve):
            def weights(g, w):
                for c in range(DC):
                    dve.wait_ge(whi_ready, g * DC + c + 1)
                    nc.vector.tensor_tensor(wlo[w][:, c, :], wraw[w][:, c, :], whi[w][:, c, :].bitcast(F32),
                                            ALU.subtract).then_inc(wlo_ready, 1)

            def norms(turn, u, tile, cos, sin):
                n = turn * U + u
                half = HD // 2
                dve.wait_ge(std_ready, n + 1)
                nc.vector.reciprocal(rstd[:, u, :], std[:, u, :]).then_inc(rstd_ready, 1)
                if not is_first(n, 2):
                    dve.wait_ge(turned_ready, n - 1)
                c = cos[:, bass.ds(tile, 1), :].to_broadcast([P, G4, HD])
                s = sin[:, bass.ds(tile, 1), :].to_broadcast([P, G4, HD])
                nc.vector.tensor_tensor(straight[u % 2][:], psP[u][:], c, ALU.mult)
                nc.vector.tensor_tensor(crossed[u % 2][:, :, 0:half], psP[u][:, :, half:HD], s[:, :, 0:half], ALU.mult)
                nc.vector.tensor_tensor(crossed[u % 2][:, :, half:HD], psP[u][:, :, 0:half], s[:, :, half:HD], ALU.mult)\
                    .then_inc(parts_ready, 1)

            def chunk(g, w, cos, sin, peel=False):
                weights(g + 1, 1 - w)
                if peel:
                    for u in range(U):
                        norms(0, u, u, cos, sin)
                with dve.Fori(1 if peel else 0, NT // U) as k:
                    for u in range(U):
                        norms(g * (NT // U) + k, u, k * U + u, cos, sin)

            weights(0, 0)
            chunk(0, 0, t["cosq"], t["sinq"], True)
            chunk(1, 1, t["cosq"], t["sinq"])
            with dve.Fori(1, NQ // 2) as pair:
                for w in range(2):
                    chunk(pair * 2 + w, w, t["cosq"], t["sinq"])
            for w in range(2):
                chunk(NQ + w, w, t["cosk"], t["sink"])
            weights(NG - 1, 1)


def attention(nc, t, d):
    ROWS = REP * S
    NH = HK
    STEPS = BT * NH
    NG = NT
    SPLIT = NH
    AHEAD = 5
    TURNED = 2
    NPB = NPP + 1
    CH = L // P
    QUADS = STEPS // G4
    W = L + S
    HW = W // 2
    with ExitStack() as ctx:
        def sb(name, shape, dt=F32):
            return ctx.enter_context(nc.sbuf_tensor(name, shape, dt))

        def ps(name, shape):
            return ctx.enter_context(nc.psum_tensor(name, shape, F32))

        def sem(name):
            return ctx.enter_context(nc.semaphore(name))

        kst = [t["kst0"], sb("kst1", [P, NPB, HK, PSIZE])]
        khi = sb("khi", [P, HK, W], F32R)
        klo = sb("klo", [P, HK, W], F32R)
        vst = [t["vst0"], sb("vst1", [P, CH, HK * HD])]
        qst = [sb(f"qst{i}", [P, HK * ROWS]) for i in range(2)]
        qhi = [sb(f"qhi{i}", [P, HK * ROWS], F32R) for i in range(2)]
        qlo = [sb(f"qlo{i}", [P, HK * ROWS], F32R) for i in range(2)]
        vnew = sb("vnew", [P, HK // G4, G4, HD])
        rows = [sb(f"rows{i}", [P, CH], I32) for i in range(2)]
        mask = [sb(f"mask{i}", [P, W]) for i in range(2)]
        negm = sb("negm3", [P, NH])
        tot = sb("tot3", [P, NH])
        rtot = sb("rtot3", [P, NH])
        p_sb = sb("p_sb", [P, NH, W])
        pn_sb = sb("pn_sb", [P, NH, S])
        pT = [sb(f"pT{i}", [P, L]) for i in range(4)]
        pTn = [sb(f"pTn{i}", [P, ROWS]) for i in range(2)]
        oT = [sb(f"oT{i}", [P, G4 * ROWS]) for i in range(2)]

        psS = [ps(f"psS{i}", [P, 2, 512]) for i in range(2)]
        psN = psS[1][:, 0, HW:HW + ROWS]
        psT = [ps(f"psTp{i}", [P, L]) for i in range(2)]
        psO = [ps(f"psO{i}", [P, G4, ROWS]) for i in range(2)]

        k_in = [t["k_in0"], sem("a_k_in1")]
        q_in = [sem(f"a_q_in{i}") for i in range(2)]
        v_in = [t["v_in0"], sem("a_v_in1")]
        vnew_in = sem("a_vnew_in")
        zeroed = sem("a_zeroed")
        rows_ready = sem("a_rows_ready")
        khi_ready = sem("a_khi_ready")
        klo_ready = sem("a_klo_ready")
        qhi_ready = sem("a_qhi_ready")
        qlo_ready = sem("a_qlo_ready")
        mask_ready = sem("a_mask_ready")
        s_mm = sem("a_s_mm")
        s_ready = sem("a_s_ready")
        e_ready = sem("a_e_ready")
        r_ready = sem("a_r_ready")
        p_ready = sem("a_p_ready")
        pT_mm = sem("a_pT_mm")
        pT_ready = sem("a_pT_ready")
        pTn_mm = sem("a_pTn_mm")
        pTn_ready = sem("a_pTn_ready")
        pv_mm = sem("a_pv_mm")
        oT_ready = sem("a_oT_ready")
        oT_out = [sem(f"a_oT_out{i}") for i in range(2)]

        block = ctx.enter_context(nc.Block())

        def zero(x, n=1):
            return isinstance(x, int) and x < n

        def groups(eng, body):
            body(0, False)
            with eng.Fori(1, NG - 1) as g:
                body(g, False)
            body(NG - 1, True)

        @block.sync
        def _(sp):
            pages = [sp.alloc_register(f"page{k}") for k in range(NPP)]
            used = sp.alloc_register("used")
            sp.reg_mov(used, 0)

            def batch(g, j, early=False):
                b, i = g * BT + j, j % 2
                if not early:
                    sp.reg_add(used, used, NH)
                    sp.wait_ge(zeroed, 1)
                    sp.wait_ge(klo_ready, used)
                if not zero(b):
                    sp.load(pages, d["table"].rearrange("(o n) -> o n", o=1)[:, bass.ds(b * NPP, NPP)])
                    for k in range(NPP):
                        page = sp.snap(pages[k], min_val=0, max_val=PAGES - 1)
                        sp.dma_start(kst[i][:, k, :, :].rearrange("p h n -> p (h n)"),
                                     d["kT"][bass.ds(page, 1), :, :].rearrange("a p n -> (a p) n")).then_inc(k_in[i], 16)
                sp.dma_start(kst[i][:, NPP, :, :].rearrange("p h n -> p (h n)"),
                             d["kTn"][bass.ds(b, 1), :, :].rearrange("a p n -> (a p) n")).then_inc(k_in[i], 16)
                if not early:
                    sp.wait_ge(qlo_ready, b - 1)
                sp.dma_start(qst[i][:], d["qT"][bass.ds(b, 1), :, :].rearrange("a p n -> (a p) n")).then_inc(q_in[i], 16)

            def new_values(g, j):
                b = g * BT + j
                if not zero(b):
                    sp.wait_ge(pv_mm, b * NH)
                src = d["vn"].rearrange("(b s) (q h n) -> h b s q n", s=S, q=HK // G4, h=G4)
                for h in range(G4):
                    sp.dma_start(vnew[h * S:(h + 1) * S, :, h, :],
                                 src[h, bass.ds(b, 1), :, :, :].rearrange("a s q n -> (a s) q n")).then_inc(vnew_in, 16)

            batch(0, 0, True)
            batch(0, 1, True)
            sp.wait_ge(zeroed, 1)
            new_values(0, 0)
            batch(0, 2)
            new_values(0, 1)
            batch(0, 3)
            new_values(0, 2)
            for k in range(HQ // 2 // WO_PIECE):
                heads = slice(k * WO_PIECE, (k + 1) * WO_PIECE)
                sp.dma_start(t["wo_first"][:, heads, :].rearrange("p h n -> p (h n)"),
                             d["wo"][:, heads, :].rearrange("p h n -> p (h n)")).then_inc(t["wo_first_in"], 16)
            with sp.Fori(1, NG) as g:
                for j in range(BT):
                    batch(g, j)
                    new_values(g, j - 1)
            new_values(NG, -1)

        @block.gpsimd
        def _(pool):
            nc.gpsimd.memset(vnew[:], 0.0).then_inc(zeroed, 1)
            copied = pool.alloc_register("copied")
            pool.reg_mov(copied, 0)

            def values(g, j, early=False):
                b, i = g * BT + j, j % 2
                if not early:
                    pool.wait_ge(pv_mm, b * NH - NH)
                nc.gpsimd.tensor_copy(rows[i][:], t["vrows"][:, bass.ds(b, 1), :].rearrange("p a c -> p (a c)"))\
                    .then_inc(rows_ready, 1)
                pool.reg_add(copied, copied, 1)
                pool.wait_ge(zeroed, 1)
                pool.wait_ge(rows_ready, copied)
                gather(i, 0)

            def gather(i, c):
                nc.gpsimd.indirect_dma_start(vst[i][:, c, :], None, d["v"],
                                             bass.IndirectOffsetOnAxis(rows[i][:, c:c + 1], 0)).then_inc(v_in[i], 16)

            def low(g, l):
                m, i, h = g * STEPS + l, l // NH % 2, l % NH
                pool.wait_ge(khi_ready, m + 1)
                nc.gpsimd.tensor_tensor(klo[:, h, :].rearrange("p (k n) -> p k n", n=PSIZE), kst[i][:, :, h, :],
                                        khi[:, h, :].rearrange("p (k n) -> p k n", n=PSIZE).bitcast(F32), ALU.subtract)\
                    .then_inc(klo_ready, 1)

            for l in range(SPLIT):
                low(0, l)
            values(0, 1, True)
            for c in range(1, CH):
                gather(1, c)

            def group(g, last):
                for l in range(STEPS):
                    if l + SPLIT < STEPS or not last:
                        low(g, l + SPLIT)
                    if (l // NH + 1 < BT or not last) and not zero(g * STEPS + l, NH):
                        if l % NH == 0:
                            values(g, l // NH + 1)
                        elif l % NH < CH:
                            gather((l // NH + 1) % 2, l % NH)

            groups(pool, group)

        @block.tensor
        def _(pe):
            def scores(g, l):
                m, i, h = g * STEPS + l, l // NH % 2, l % NH
                if not zero(m, 2):
                    pe.wait_ge(s_ready, m - 1)
                if l % G4 == G4 - 1 and not zero(m, G4):
                    pe.wait_ge(pTn_ready, g * QUADS + l // G4)
                if h == 0:
                    pe.wait_ge(qlo_ready, g * BT + l // NH + 1)
                pe.wait_ge(klo_ready, m + 1)
                qs = slice(h * ROWS, (h + 1) * ROWS)
                for k in range(2):
                    ks = slice(k * HW, (k + 1) * HW)
                    mm = split3(pe, psS[l % 2][:, k, 0:HW], (qhi[i][:, qs], qlo[i][:, qs]),
                                (khi[:, h, ks], klo[:, h, ks]), True, True)
                mm.then_inc(s_mm, 1)

            def transposes(g, l, last=False):
                m = g * STEPS + l
                pe.wait_ge(p_ready, m + 1)
                if not zero(m, 2):
                    pe.wait_ge(pT_ready, m - 1)
                for c in range(CH):
                    mm = pe.transpose(psT[l % 2][:, c * P:(c + 1) * P], p_sb[:, l % NH, c * P:(c + 1) * P], t["ident"][:])
                mm.then_inc(pT_mm, 1)
                if l % G4 == G4 - 1:
                    pe.wait_ge(s_ready, m + 1 if last and l == STEPS - 1 else m + 3)
                    first = l % NH - G4 + 1
                    pe.transpose(psN, pn_sb[:, first:first + G4, :].rearrange("p h s -> p (h s)"),
                                 t["ident"][:]).then_inc(pTn_mm, 1)

            def products(g, l):
                m, i, h = g * STEPS + l, l // NH % 2, l % NH
                quad = g * QUADS + l // G4
                turn = g * (BT // 2) + l // NH // 2 + 1
                out = psO[l // G4 % 2]
                if h == 0:
                    pe.wait_ge(v_in[i], 16 * CH * turn)
                if l % G4 == 0 and not zero(quad, 2):
                    pe.wait_ge(oT_ready, quad - 1)
                pe.wait_ge(pT_ready, m + 1)
                for c in range(CH):
                    mm = pe.matmul(out[:, l % G4, :], vst[i][:, c, h * HD:(h + 1) * HD], pT[l % 4][:, c * P:(c + 1) * P],
                                   start=(l % G4 == 0 and c == 0), stop=False, skip_group_check=True)
                if l % G4 == G4 - 1:
                    pe.wait_ge(pTn_ready, quad + 1)
                    if h == G4 - 1:
                        pe.wait_ge(vnew_in, 16 * G4 * (g * BT + l // NH + 1))
                    for k in range(G4):
                        mm = pe.matmul(out[:, k, :], vnew[:, h // G4, k, :], pTn[l // G4 % 2][:],
                                       start=False, stop=(k == G4 - 1), skip_group_check=True)
                mm.then_inc(pv_mm, 1)

            for l in range(AHEAD):
                scores(0, l)
            for l in range(TURNED):
                transposes(0, l)

            def group(g, last):
                for l in range(STEPS):
                    if l + AHEAD < STEPS or not last:
                        scores(g, l + AHEAD)
                    if l + TURNED < STEPS or not last:
                        transposes(g, l + TURNED, last)
                    products(g, l)

            groups(pe, group)

        @block.scalar
        def _(act):
            def queries(g, j):
                b, i = g * BT + j, j % 2
                act.wait_ge(q_in[i], 16 * (g * (BT // 2) + j // 2 + 1))
                if not zero(b, 2):
                    act.wait_ge(s_mm, b * NH - NH)
                nc.scalar.activation(qhi[i][:], qst[i][:], ACT.Copy).then_inc(qhi_ready, 1)

            def high(g, l):
                m, i, h = g * STEPS + l, l // NH % 2, l % NH
                if h == 0:
                    act.wait_ge(k_in[i], 16 * NPB * (g * (BT // 2) + l // NH // 2 + 1))
                if not zero(m, NH):
                    act.wait_ge(s_mm, m - NH + 1)
                nc.scalar.activation(khi[:, h, :].rearrange("p (k n) -> p k n", n=PSIZE), kst[i][:, :, h, :], ACT.Copy)\
                    .then_inc(khi_ready, 1)

            def exps(g, l):
                m, h = g * STEPS + l, l % NH
                act.wait_ge(s_ready, m + 1)
                nc.scalar.activation(p_sb[:, h, :], p_sb[:, h, :], ACT.Exp, bias=negm[:, h:h + 1], scale=-1.0,
                                     accum_out=tot[:, h:h + 1]).then_inc(e_ready, 1)

            def probs_out(g, l):
                m = g * STEPS + l
                act.wait_ge(pT_mm, m + 1)
                if not zero(m, 4):
                    act.wait_ge(pv_mm, m - 3)
                nc.scalar.activation(pT[l % 4][:], psT[l % 2][:], ACT.Copy).then_inc(pT_ready, 1)
                if l % G4 == G4 - 1:
                    quad = g * QUADS + l // G4
                    act.wait_ge(pTn_mm, quad + 1)
                    if not zero(quad, 2):
                        act.wait_ge(pv_mm, (quad - 1) * G4)
                    nc.scalar.activation(pTn[l // G4 % 2][:], psN, ACT.Copy).then_inc(pTn_ready, 1)

            queries(0, 0)
            high(0, 0)
            high(0, 1)
            for l in range(AHEAD - 1):
                high(0, l + 2)
                exps(0, l)
            for k in range(TURNED):
                probs_out(0, k)
                high(0, AHEAD + 1 + k)

            def group(g, last):
                for l in range(STEPS):
                    if l + AHEAD - 1 < STEPS or not last:
                        exps(g, l + AHEAD - 1)
                    if l + SPLIT < STEPS or not last:
                        high(g, l + SPLIT)
                    if l + TURNED < STEPS or not last:
                        probs_out(g, l + TURNED)
                    if l % NH == 1 and (l // NH + 1 < BT or not last):
                        queries(g, l // NH + 1)
                    if l % G4 == 1 and not zero(g * STEPS + l, G4):
                        send(g, l // G4 - 1)

            def send(g, q):
                quad = g * QUADS + q
                i = q % 2
                act.wait_ge(oT_ready, quad + 1)
                dst = d["oT"].rearrange("(t j) p (q n) -> t p j q n", j=BT, q=2)
                tile = g + q // QUADS
                act.dma_start(dst[bass.ds(tile, 1), :, q // 2 % BT, i, :].rearrange("a p n -> (a p) n"), oT[i][:])\
                    .then_inc(oT_out[i], 16)

            groups(act, group)
            send(NG - 1, QUADS - 1)
            for i in range(2):
                act.wait_ge(oT_out[i], 16 * NG * QUADS // 2)

        @block.vector
        def _(dve):
            def queries(g, j):
                b, i = g * BT + j, j % 2
                dve.wait_ge(qhi_ready, b + 1)
                nc.vector.tensor_tensor(qlo[i][:], qst[i][:], qhi[i][:].bitcast(F32), ALU.subtract).then_inc(qlo_ready, 1)
                if not zero(b, 2):
                    dve.wait_ge(s_ready, b * NH - NH)
                nc.vector.tensor_scalar(mask[i][:, 0:L], t["key_no"][:],
                                        t["cached"][:, bass.ds(b, 1)], MASKED, ALU.is_ge, ALU.mult).then_inc(mask_ready, 1)

            def scores_done(g, l):
                m, h = g * STEPS + l, l % NH
                if h == 0:
                    dve.wait_ge(mask_ready, g * BT + l // NH + 2)
                if not zero(m, NH):
                    dve.wait_ge(pTn_mm, g * QUADS + l // G4 - 1)
                dve.wait_ge(s_mm, m + 1)

            def least(g, l):
                i, h = l // NH % 2, l % NH
                nc.vector.tensor_tensor_reduce(out=p_sb[:, h, :].rearrange("p (k n) -> p k n", k=2),
                                               in0=psS[l % 2][:, :, 0:HW],
                                               in1=mask[i][:].rearrange("p (k n) -> p k n", k=2), scale=-SCALE,
                                               scalar=BIG, op0=ALU.add, op1=ALU.min,
                                               accum_out=negm[:, h:h + 1]).then_inc(s_ready, 1)

            def norm(g, l):
                m, h = g * STEPS + l, l % NH
                dve.wait_ge(e_ready, m + 1)
                nc.vector.reciprocal(rtot[:, h:h + 1], tot[:, h:h + 1]).then_inc(r_ready, 1)
                dve.wait_ge(r_ready, m + 1)
                nc.vector.tensor_scalar(p_sb[:, h, 0:L], p_sb[:, h, 0:L], rtot[:, h:h + 1], None, ALU.mult)

            def norm_new(g, l):
                h = l % NH
                nc.vector.tensor_scalar(pn_sb[:, h, :], p_sb[:, h, L:W], rtot[:, h:h + 1], None, ALU.mult)\
                    .then_inc(p_ready, 1)

            def output(g, q):
                quad = g * QUADS + q
                dve.wait_ge(pv_mm, (quad + 1) * G4)
                if not zero(quad, 2):
                    dve.wait_ge(oT_out[q % 2], 16 * (g * (QUADS // 2) + q // 2))
                nc.vector.tensor_copy(oT[q % 2][:], psO[q % 2][:].rearrange("p k r -> p (k r)")).then_inc(oT_ready, 1)

            nc.vector.memset(mask[0][:, L:W], 0.0)
            nc.vector.memset(mask[1][:, L:W], 0.0).then_inc(mask_ready, 1)
            queries(0, 0)
            for l in range(AHEAD):
                if l > 1:
                    norm(0, l - 2)
                    norm_new(0, l - 2)
                scores_done(0, l)
                least(0, l)

            def group(g, last):
                for l in range(STEPS):
                    ahead = l + AHEAD < STEPS or not last
                    if l + AHEAD - 2 < STEPS or not last:
                        norm(g, l + AHEAD - 2)
                        if ahead:
                            scores_done(g, l + AHEAD)
                        norm_new(g, l + AHEAD - 2)
                    if ahead:
                        least(g, l + AHEAD)
                    if l % G4 == 0 and not zero(g * STEPS + l):
                        output(g, l // G4 - 1)
                    if l % NH == 1 and (l // NH + 1 < BT or not last):
                        queries(g, l // NH + 1)

            groups(dve, group)
            output(NG - 1, QUADS - 1)


def output_ffn(nc, t, d):
    PARTS = 4
    HP = HQ // PARTS
    HR = HQ // 2
    WR = WO_PIECE
    with ExitStack() as ctx:
        def sb(name, shape, dt=F32):
            return ctx.enter_context(nc.sbuf_tensor(name, shape, dt))

        def ps(name, shape):
            return ctx.enter_context(nc.psum_tensor(name, shape, F32))

        def sem(name):
            return ctx.enter_context(nc.semaphore(name))

        wohi = sb("wohi", [P, HQ, D], F32R)
        place = [t["wo_first_at"], nc.sbuf_base]
        wo = [t["wo_first"], sb("wo_second", [P, HQ // 2, D])]
        wolo = [nc.alloc_sbuf_tensor_at(f"wolo{i}", [P, HQ // 2, D], F32R, offset=place[i]) for i in range(2)]
        raw = [sb(f"raw{i}", [P, HR * P]) for i in range(2)]
        oThi = sb("oThi", [P, HQ, P], F32R)
        oTlo = sb("oTlo", [P, HQ, P], F32R)
        wb = sb("wb", [P, DC, D], F32R)
        gate = sb("gate", [P, DC, NE])
        in_sc = sb("in_sc", [NE, D])
        out_sc = sb("out_sc", [NE, D])
        bias1 = sb("bias1", [P, D])
        att = sb("att", [P, D])
        attT = sb("attT", [P, DC * P])
        zhi = sb("zhi", [P, DC * P], F32R)
        zlo = sb("zlo", [P, DC * P], F32R)
        rneg = sb("rneg", [P, 1])
        rex = sb("rex", [P, NE])
        rsum = sb("rsum", [P, 1])
        rrec = sb("rrec", [P, 1])
        route = sb("route", [P, NE])
        routeT = sb("routeT", [NE, P])
        x1b = sb("x1b", [P, D])

        psW = [ps(f"psW{i}", [P, D]) for i in range(2)]
        psF = ps("psF", [P, D])
        psZ = ps("psZ", [P, D])

        weights_in = sem("o_weights_in")
        raw_in = [sem(f"o_raw_in{i}") for i in range(2)]
        wo_in = [sem(f"o_wo_in{k}") for k in range(HR // WR)]
        wo_high = sem("o_wo_high")
        wo_low = sem("o_wo_low")
        wb_in = [sem(f"o_wb_in{i}") for i in range(2)]
        sign_ready = sem("o_sign_ready")
        oT_high = sem("o_oT_high")
        oT_low = sem("o_oT_low")
        wo_mm = sem("o_wo_mm")
        att_ready = sem("o_att_ready")
        attT_mm = sem("o_attT_mm")
        attT_ready = sem("o_attT_ready")
        logit_mm = sem("o_logit_mm")
        rneg_ready = sem("o_rneg_ready")
        rex_ready = sem("o_rex_ready")
        rrec_ready = sem("o_rrec_ready")
        route_ready = sem("o_route_ready")
        routeT_mm = sem("o_routeT_mm")
        routeT_ready = sem("o_routeT_ready")
        in_mm = sem("o_in_mm")
        z_ready = sem("o_z_ready")
        zhi_ready = sem("o_zhi_ready")
        zlo_ready = sem("o_zlo_ready")
        out_mm = sem("o_out_mm")
        osc_ready = sem("o_osc_ready")
        ffn_mm = sem("o_ffn_mm")
        scaled = sem("o_scaled")
        biased = sem("o_biased")
        fin_ready = sem("o_fin_ready")
        x1_in = sem("o_x1_in")
        fin_out = sem("o_fin_out")

        block = ctx.enter_context(nc.Block())
        NW = HQ // WR
        NH2 = NW // 2

        def piece(k):
            i, at = k // NH2, slice(k % NH2 * WR, (k % NH2 + 1) * WR)
            return [w[:, part, :].rearrange("p h n -> p (h n)")
                    for w, part in ((wo[i], at), (wohi, slice(k * WR, (k + 1) * WR)), (wolo[i], at))]

        def zero(x, n=1):
            return isinstance(x, int) and x < n

        def tiles(eng, body):
            body(0, 0)
            body(1, 1)
            with eng.Fori(1, NT // 2) as pair:
                for u in range(2):
                    body(pair * 2 + u, u)

        @block.sync
        def _(sp):
            def raw_heads(tile, i):
                src = d["oT"].rearrange("(t j) p (q n) -> t q p j n", j=BT, q=2)
                sp.dma_start(raw[i][:].rearrange("p (j n) -> p j n", j=BT),
                             src[bass.ds(tile, 1), i, :, :, :].rearrange("a p j n -> (a p) j n")).then_inc(raw_in[i], 16)

            for i in range(2):
                raw_heads(0, i)
            for k in range(NH2, NW):
                sp.dma_start(piece(k)[0], d["wo"][:, k * WR:(k + 1) * WR, :].rearrange("p h n -> p (h n)"))\
                    .then_inc(wo_in[k - NH2], 16)
            sp.dma_start(gate[:], d["gate"]).then_inc(weights_in, 16)
            sp.dma_start(in_sc[:], d["in_sc"]).then_inc(weights_in, 16)
            sp.dma_start(out_sc[:], d["out_sc"]).then_inc(weights_in, 16)
            sp.dma_start(bias1[:], d["b1"].rearrange("(o n) -> o n", o=1).to_broadcast([P, D]))\
                .then_inc(weights_in, 16)

            def sign_weights(c):
                if c >= 2:
                    sp.wait_ge(sign_ready, 2 * (c - 1))
                sp.dma_start((x1b, attT)[c % 2][:], d["wb"][:, c, :]).then_inc(wb_in[c % 2], 16)

            for c in range(2):
                sign_weights(c)

            def body(tile, u):
                for i in range(2):
                    sp.wait_ge(oT_low, tile * PARTS + 2 * i + 2)
                    raw_heads(tile + 1, i)
                if zero(tile):
                    for c in range(2, DC):
                        sign_weights(c)
                    sp.wait_ge(sign_ready, 2 * DC)
                else:
                    sp.wait_ge(fin_ready, tile)
                    sp.dma_start(d["out"][bass.ds((tile - 1) * P, P), :], att[:]).then_inc(fin_out, 16)
                sp.dma_start(x1b[:], d["x1"][bass.ds(tile * P, P), :]).then_inc(x1_in, 16)

            body(0, 0)
            with sp.Fori(1, NT - 1) as tile:
                body(tile, 0)
            sp.wait_ge(fin_ready, NT - 1)
            sp.dma_start(d["out"][(NT - 2) * P:(NT - 1) * P, :], att[:]).then_inc(fin_out, 16)
            sp.dma_start(x1b[:], d["x1"][(NT - 1) * P:NT * P, :]).then_inc(x1_in, 16)
            sp.wait_ge(fin_ready, NT)
            sp.dma_start(d["out"][(NT - 1) * P:NT * P, :], att[:]).then_inc(fin_out, 16)
            sp.wait_ge(fin_out, 16 * NT)

        @block.gpsimd
        def _(pool):
            pool.wait_ge(weights_in, 16 * 4)

            def add(tile):
                pool.wait_ge(scaled, tile + 1)
                nc.gpsimd.tensor_tensor(att[:], att[:], bias1[:], ALU.add).then_inc(biased, 1)
                pool.wait_ge(biased, tile + 1)
                pool.wait_ge(x1_in, 16 * (tile + 1))
                nc.gpsimd.tensor_tensor(att[:], att[:], x1b[:], ALU.add).then_inc(fin_ready, 1)

            add(0)
            with pool.Fori(1, NT) as tile:
                add(tile)

        @block.tensor
        def _(pe):
            def product(tile, u, k):
                if k % 4 == 0:
                    pe.wait_ge(oT_low, tile * PARTS + k // 4 + 1)
                if k == 0 and not zero(tile, 2):
                    pe.wait_ge(att_ready, tile - 1)
                if zero(tile) and k % (WR // 2) == 0:
                    pe.wait_ge(wo_low, k // (WR // 2) + 1)
                for h in (2 * k, 2 * k + 1):
                    mm = split3(pe, psW[u][:], (oThi[:, h, :], oTlo[:, h, :]),
                                (wohi[:, h, :], wolo[h // HR][:, h % HR, :]), h == 0, h == HQ - 1)
                if k % 4 == 3:
                    mm.then_inc(wo_mm, 1)

            def ffn(tile, k):
                if k == 1:
                    pe.wait_ge(att_ready, tile + 1)
                    if not zero(tile):
                        pe.wait_ge(osc_ready, tile)
                    for c in range(DC):
                        mm = pe.transpose(psF[:, c * P:(c + 1) * P], att[:, c * P:(c + 1) * P], t["ident"][:])
                    mm.then_inc(attT_mm, 1)
                if k == 3:
                    pe.wait_ge(attT_ready, tile + 1)
                    for c in range(DC):
                        mm = pe.matmul(psF[:, 0:NE], attT[:, c * P:(c + 1) * P], gate[:, c, :],
                                       start=(c == 0), stop=(c == DC - 1))
                    mm.then_inc(logit_mm, 1)
                if k == 6:
                    pe.wait_ge(route_ready, tile + 1)
                    pe.transpose(psF[0:NE, 0:P], route[:], t["ident"][:]).then_inc(routeT_mm, 1)
                if k == 8:
                    pe.wait_ge(routeT_ready, tile + 1)
                    for c in range(DC):
                        mm = pe.matmul(psF[:, c * P:(c + 1) * P], in_sc[:, c * P:(c + 1) * P], routeT[:],
                                       start=True, stop=True)
                    mm.then_inc(in_mm, 1)
                if k == 11:
                    if zero(tile):
                        pe.wait_ge(sign_ready, 2 * DC)
                    pe.wait_ge(zlo_ready, tile + 1)
                    pe.matmul(psF[:], routeT[:], out_sc[:], start=True, stop=True).then_inc(out_mm, 1)
                    if not zero(tile):
                        pe.wait_ge(scaled, tile)
                    for c in range(DC):
                        pe.matmul(psZ[:], zhi[:, c * P:(c + 1) * P], wb[:, c, :], start=(c == 0), stop=False)
                        mm = pe.matmul(psZ[:], zlo[:, c * P:(c + 1) * P], wb[:, c, :], start=False, stop=(c == DC - 1))
                    mm.then_inc(ffn_mm, 1)

            for k in range(16):
                product(0, 0, k)
            pe.wait_ge(weights_in, 16 * 4)

            def body(tile, u):
                for k in range(16):
                    product(tile, u, k)
                    ffn(tile - 1, k)

            body(1, 1)
            with pe.Fori(1, NT // 2) as pair:
                for u in range(2):
                    body(pair * 2 + u, u)
            for k in range(12):
                ffn(NT - 1, k)

        @block.scalar
        def _(act):
            def weights(k):
                if k < NH2:
                    act.wait_ge(t["wo_first_in"], 16 * NH2)
                else:
                    act.wait_ge(wo_in[k - NH2], 16)
                src, high_part, _ = piece(k)
                nc.scalar.activation(high_part, src, ACT.Copy).then_inc(wo_high, 1)

            def high(tile, u, q):
                i = q // 2
                if q % 2 == 0:
                    act.wait_ge(raw_in[i], 16 * (tile + 1))
                if not zero(tile):
                    act.wait_ge(wo_mm, (tile - 1) * PARTS + q + 1)
                src = raw[i][:].rearrange("p (j h s) -> p j h s", j=BT, s=S)[:, :, (q % 2) * HP:(q % 2 + 1) * HP, :]
                for j in range(BT):
                    ins = nc.scalar.activation(oThi[:, q * HP:(q + 1) * HP, j * S:(j + 1) * S], src[:, j, :, :], ACT.Copy)
                ins.then_inc(oT_high, 1)

            def ffn(tile, u, k):
                if k == 0:
                    act.wait_ge(wo_mm, (tile + 1) * PARTS)
                    if zero(tile):
                        act.wait_ge(sign_ready, 2 * DC)
                    if not zero(tile):
                        act.wait_ge(fin_out, 16 * tile)
                    nc.scalar.activation(att[:], psW[u][:], ACT.Copy).then_inc(att_ready, 1)
                if k == 1:
                    act.wait_ge(attT_mm, tile + 1)
                    if not zero(tile):
                        act.wait_ge(zlo_ready, tile)
                    nc.scalar.activation(attT[:], psF[:], ACT.Copy).then_inc(attT_ready, 1)
                if k == 2:
                    act.wait_ge(rneg_ready, tile + 1)
                    nc.scalar.activation(rex[:], psF[:, 0:NE], ACT.Exp, bias=rneg[:, 0:1], accum_out=rsum[:, 0:1])\
                        .then_inc(rex_ready, 1)
                if k == 3:
                    act.wait_ge(routeT_mm, tile + 1)
                    nc.scalar.activation(routeT[:], psF[0:NE, 0:P], ACT.Copy).then_inc(routeT_ready, 1)
                if k == 4:
                    act.wait_ge(z_ready, tile + 1)
                    if not zero(tile):
                        act.wait_ge(ffn_mm, tile)
                    nc.scalar.activation(zhi[:], attT[:], ACT.Copy).then_inc(zhi_ready, 1)
                if k == 5:
                    act.wait_ge(out_mm, tile + 1)
                    nc.scalar.activation(att[:], psF[:], ACT.Copy).then_inc(osc_ready, 1)

            after = {0: 1, 1: 3, 2: 4, 3: 5}
            for q in range(PARTS):
                high(0, 0, q)
                for k in range(q * NW // PARTS, (q + 1) * NW // PARTS):
                    weights(k)
            for q in range(PARTS):
                high(1, 1, q)

            def body(tile, u):
                for k in range(6):
                    ffn(tile, u, k)
                    for q in range(PARTS):
                        if after[q] == k and not (isinstance(tile, int) and tile >= NT - 2):
                            high(tile + 2, u, q)

            body(0, 0)
            body(1, 1)
            with act.Fori(1, NT // 2 - 1) as pair:
                for u in range(2):
                    body(pair * 2 + u, u)
            body(NT - 2, 0)
            body(NT - 1, 1)

        @block.vector
        def _(dve):
            def weights(k):
                dve.wait_ge(wo_high, k + 1)
                src, high_part, low_part = piece(k)
                nc.vector.tensor_tensor(low_part, src, high_part.bitcast(F32), ALU.subtract).then_inc(wo_low, 1)

            def low(tile, q):
                i = q // 2
                dve.wait_ge(oT_high, tile * PARTS + q + 1)
                src = raw[i][:].rearrange("p (j h s) -> p j h s", j=BT, s=S)[:, :, (q % 2) * HP:(q % 2 + 1) * HP, :]
                for j in range(BT):
                    at = (slice(None), slice(q * HP, (q + 1) * HP), slice(j * S, (j + 1) * S))
                    ins = nc.vector.tensor_tensor(oTlo[at], src[:, j, :, :], oThi[at].bitcast(F32), ALU.subtract)
                ins.then_inc(oT_low, 1)

            for q in range(PARTS):
                low(0, q)
                for k in range(q * NW // PARTS, (q + 1) * NW // PARTS):
                    weights(k)
            for q in range(PARTS):
                low(1, q)
            for c in range(DC):
                dve.wait_ge(wb_in[c % 2], 16 * (c // 2 + 1))
                src = (x1b, attT)[c % 2]
                nc.vector.tensor_scalar(att[:], src[:], 0.0, None, ALU.is_lt).then_inc(sign_ready, 1)
                dve.wait_ge(sign_ready, 2 * c + 1)
                nc.vector.scalar_tensor_tensor(out=wb[:, c, :], in0=src[:], scalar=0.0, in1=att[:],
                                               op0=ALU.is_gt, op1=ALU.subtract).then_inc(sign_ready, 1)
                dve.wait_ge(sign_ready, 2 * c + 2)

            def ffn(tile, k):
                if k == 2:
                    dve.wait_ge(logit_mm, tile + 1)
                    nc.vector.tensor_reduce(rneg[:], psF[:, 0:NE], AX.X, ALU.max, negate=True).then_inc(rneg_ready, 1)
                    dve.wait_ge(rex_ready, tile + 1)
                    nc.vector.reciprocal(rrec[:], rsum[:]).then_inc(rrec_ready, 1)
                    dve.wait_ge(rrec_ready, tile + 1)
                    nc.vector.tensor_scalar(route[:], rex[:], rrec[:, 0:1], None, ALU.mult).then_inc(route_ready, 1)
                if k == 3:
                    dve.wait_ge(in_mm, tile + 1)
                    nc.vector.tensor_tensor(attT[:], psF[:], attT[:], ALU.mult).then_inc(z_ready, 1)
                if k == 4:
                    dve.wait_ge(zhi_ready, tile + 1)
                    nc.vector.tensor_tensor(zlo[:], attT[:], zhi[:].bitcast(F32), ALU.subtract).then_inc(zlo_ready, 1)
                if k == 5:
                    dve.wait_ge(ffn_mm, tile + 1)
                    dve.wait_ge(osc_ready, tile + 1)
                    nc.vector.tensor_tensor(att[:], psZ[:], att[:], ALU.mult).then_inc(scaled, 1)

            after = {0: 2, 1: 3, 2: 4, 3: 5}

            def body(tile, u):
                for k in range(2, 6):
                    ffn(tile, k)
                    for q in range(PARTS):
                        if after[q] == k and not (isinstance(tile, int) and tile >= NT - 2):
                            low(tile + 2, q)

            body(0, 0)
            body(1, 1)
            with dve.Fori(1, NT // 2 - 1) as pair:
                for u in range(2):
                    body(pair * 2 + u, u)
            body(NT - 2, 0)
            body(NT - 1, 1)


def adaln_ffn_program(nc, d):
    with ExitStack() as ctx:
        def sb(name, shape, dt=F32):
            return ctx.enter_context(nc.sbuf_tensor(name, shape, dt))

        t = {
            "ident": sb("ident", [P, P]),
            "cached": sb("cached", [P, B]),
            "key_no": sb("key_no", [P, L], mybir.dt.float16),
            "vrows": sb("vrows", [P, B, G4], I32),
        }
        far = ctx.enter_context(ExitStack())
        with ExitStack() as early:
            def sbe(name, shape, dt=F32):
                return early.enter_context(nc.sbuf_tensor(name, shape, dt))

            t["xThi"] = sbe("xThi", [P, DC, B * S], F32R)
            t["xTlo"] = sbe("xTlo", [P, DC, B * S], F32R)
            for name in ("cosq", "sinq", "cosk", "sink"):
                t[name] = sbe(name, [P, NT, HD])
            t["wraw"] = [sbe(f"wraw{i}", [P, DC, D]) for i in range(2)]
            t["wraw_in"] = [early.enter_context(nc.semaphore(f"wraw_in{i}")) for i in range(2)]
            with ExitStack() as first:
                def sbf(name, shape, dt=F32):
                    return first.enter_context(nc.sbuf_tensor(name, shape, dt))

                t["w2"] = sbf("w2", [P, 2 * S])
                t["b2"] = sbf("b2", [P, S])
                t["bs"] = sbf("bs", [8, 2, HID])
                t["bias0"] = sbf("bias0", [P, D])
                t["freq"] = sbf("freq", [P, HD // 2])
                t["qw"] = sbf("qw", [P, HD])
                t["kw"] = sbf("kw", [P, HD])
                t["onehot"] = sbf("onehot", [8, B])
                t["wrows"] = sbf("wrows", [P, NT], I32)
                t["wsel"] = sbf("wsel", [P, NT, HID])
                t["seen4"] = sbf("seen4", [P, NT, BT])
                t["tmask"] = sbf("tmask", [P, DC, B])
                t["pos"] = sbf("pos", [P, NT])
                for name in ("part", "sin", "cos"):
                    t[name] = sbf(name, [P, NT, HD // 2])
                t["yT"] = sbf("yT", [P, DC, B * S])
                t["w0"] = sbf("w0", [P, DC, D])
                t["wqk"] = sbf("wqk", [P, DC, 2, NE * DK])
                t["wa"] = sbf("wa", [P, DC, NE * RANK])
                t["bm"] = sbf("bm", [NE * RANK, D])
                t["small_in"] = first.enter_context(nc.semaphore("small_in"))
                t["smalls"] = 9
                t["weights_in"] = first.enter_context(nc.semaphore("weights_in"))
                tables(nc, t, d)
                sessions(nc, t, d)
                layer0(nc, t, d)
            t["kst0"] = far.enter_context(nc.sbuf_tensor("kst0", [P, NPP + 1, HK, PSIZE], F32, side="right"))
            t["vst0"] = far.enter_context(nc.sbuf_tensor("vst0", [P, L // P, HK * HD], F32, side="right"))
            t["k_in0"] = far.enter_context(nc.semaphore("k_in0"))
            t["v_in0"] = far.enter_context(nc.semaphore("v_in0"))
            projections(nc, t, d)
        t["wo_first_at"] = nc.sbuf_base
        t["wo_first"] = sb("wo_first", [P, HQ // 2, D])
        t["wo_first_in"] = ctx.enter_context(nc.semaphore("wo_first_in"))
        attention(nc, t, d)
        far.close()
        output_ffn(nc, t, d)


def kernel(**inputs):
    import concourse.bacc as bacc
    from concourse.bass_utils import run_bass_kernel_spmd

    def flat(name, shape):
        return np.asarray(inputs[name]).reshape(shape)

    def by_chunk(w):
        w = np.asarray(w)
        return w.T.reshape(-1, P, w.shape[0]).transpose(1, 0, 2)

    wqkv = np.concatenate([np.asarray(inputs[f"L1_cond_{n}"]) for n in ("Wq", "Wk", "Wv")])
    freq = (1.0 / np.float32(THETA) ** (np.arange(0, HD, 2, dtype=np.float32) / np.float32(HD))).astype(np.float32)
    arrays = {
        "x": flat("x", (B * S, D)),
        "ids": flat("itok_B_0_7", (B,)),
        "frames": flat("itok_B_2182_4065", (B,)),
        "table": flat("itok_Bx16_0_63", (B * NPP,)),
        "cached": flat("itok_B_207_1644", (B,)),
        "counts": flat("_lenS", (B,)),
        "freq": freq,
        "w_sess": flat("L0_cond_W_sess", (8 * S, HID)),
        "b_sess": flat("L0_cond_b_sess", (8, HID)),
        "w2": flat("L0_cond_W2", (HID, S)),
        "b2": flat("L0_cond_b2", (S,)),
        "w0": by_chunk(inputs["L0_ffn_W"]),
        "b0": flat("L0_ffn_b", (D,)),
        "wq0": by_chunk(inputs["L0_ffn_Wq"]),
        "wk0": by_chunk(inputs["L0_ffn_Wk"]),
        "wa": by_chunk(flat("L0_ffn_A", (NE * RANK, D))),
        "bm": flat("L0_ffn_Bm", (NE, D, RANK)).transpose(0, 2, 1).reshape(NE * RANK, D),
        "wqkv": wqkv.reshape(-1, D, DC, P).transpose(0, 3, 2, 1),
        "qw": flat("L1_cond_q_norm_w", (HD,)),
        "kw": flat("L1_cond_k_norm_w", (HD,)),
        "kT": flat("L1_cond_k_cache", (PAGES, PSIZE, HK, HD)).transpose(0, 3, 2, 1).reshape(PAGES, HD, HK * PSIZE),
        "v": flat("L1_cond_v_cache", (PAGES * PSIZE, HK * HD)),
        "wo": flat("L1_cond_Wo", (D, HQ, HD)).transpose(2, 1, 0),
        "wb": by_chunk(inputs["L1_ffn_weight"]),
        "b1": flat("L1_ffn_bias", (D,)),
        "gate": by_chunk(inputs["L1_ffn_gate_w"]),
        "in_sc": flat("L1_ffn_in_channel_scale", (NE, D)),
        "out_sc": flat("L1_ffn_out_channel_scale", (NE, D)),
    }
    arrays = {name: np.ascontiguousarray(a) for name, a in arrays.items()}
    nc = bacc.Bacc("TRN2", target_bir_lowering=False, num_devices=1)
    d = {name: nc.dram_tensor(name + "_dram", a.shape, mybir.dt.from_np(a.dtype), kind="ExternalInput").ap()
         for name, a in arrays.items()}
    for name, shape in (("x1", (B * S, D)), ("qT", (B, HD, HQ * S)), ("kTn", (B, HD, HK * S)),
                        ("vn", (B * S, HK * HD)), ("oT", (B, HD, HQ * S))):
        d[name] = nc.dram_tensor(name + "_dram", shape, F32, kind="Internal").ap()
    d["out"] = nc.dram_tensor("out_dram", (B * S, D), F32, kind="ExternalOutput").ap()
    adaln_ffn_program(nc, d)
    result = run_bass_kernel_spmd(nc, [{name + "_dram": a for name, a in arrays.items()}], core_ids=[0])
    return result.results[0]["out_dram"].reshape(B, S, D)
```
